# Optimizing a Trainium2 kernel written in Bass

```python
import numpy as np
import jax
import jax.numpy as jnp

def _softmax(x, axis=-1):
    return jax.nn.softmax(x, axis=axis)

def _gelu(x):
    return jax.nn.gelu(x, approximate=True)

def _silu(x):
    return jax.nn.silu(x)

def _sigmoid(x):
    return jax.nn.sigmoid(x)

def _layernorm(x, axis=-1, eps=1e-05):
    m = jnp.mean(x, axis=axis, keepdims=True)
    v = jnp.var(x, axis=axis, keepdims=True)
    return (x - m) / jnp.sqrt(v + eps)

def _scatter_add(tgt, idx, src, axis=0):
    return tgt.at[idx].add(src)

def _segment_sum(src, seg, n):
    return jax.ops.segment_sum(src, seg, n)
kernel_name = 'mk_xattn_seq_d4_seqx_r4_ab418b'

def setup_inputs(seed: int=0):
    np.random.seed(seed)
    _w = jnp.asarray

    def _rec_inputs():
        import jax
        import jax.numpy as jnp
        _rk = jax.random.key(seed)
        x = -0.000125 + 0.9999 * jax.random.normal(jax.random.fold_in(_rk, 1), (1, 2048, 256), jnp.float32)
        _lenS = 2048 - jax.random.randint(jax.random.fold_in(_rk, 7), (1,), 0, max(1, 2048 // 4) + 1, jnp.int32)
        _lenS2 = 1601 - jax.random.randint(jax.random.fold_in(_rk, 8), (1,), 0, max(1, 1601 // 4) + 1, jnp.int32)
        _ctx_2048P = jax.random.normal(jax.random.fold_in(_rk, 11), (1, 16, 512), jnp.float32)
        _ctx_2048c = jax.random.dirichlet(jax.random.fold_in(_rk, 511), 0.3 * jnp.ones((16,), jnp.float32), (1, 1601))
        _ctx_2048t = jnp.einsum('bsk,bkd->bsd', _ctx_2048c, _ctx_2048P)
        _ctx_2048t = _ctx_2048t * jax.lax.rsqrt(jnp.mean(jnp.square(_ctx_2048t)) + 1e-12) * 0.953939
        ctx_2048 = 5.36139e-06 + 1.00015 * (_ctx_2048t + 0.3 * jax.random.normal(jax.random.fold_in(_rk, 611), (1, 1601, 512), jnp.float32))
        _validS = jnp.arange(2048)[None, :] < _lenS[:, None]
        _validS2 = jnp.arange(1601)[None, :] < _lenS2[:, None]
        _causal = jnp.tril(jnp.ones((2048, 2048), dtype=bool))
        mask_S_fk1 = jnp.where(_validS[0], 1.0, 0.0).astype(jnp.float32)
        mask_S_fk0 = jnp.where(_validS[0], 0.0, 1.0).astype(jnp.float32)
        return (x, ctx_2048, mask_S_fk1, mask_S_fk0)
    x, ctx_2048, mask_S_fk1, mask_S_fk0 = _rec_inputs()

    def _L0_xattn_setup():
        import jax, jax.numpy as jnp
        import numpy as np
        HEADS = 16
        HEAD_DIM = 64
        SUPPRESS = 20.0
        key = jax.random.key(seed)
        ks = jax.random.split(key, 8)
        B, HW, C, T, CT = (8, 1024, 256, 77, 512)
        inner = HEADS * HEAD_DIM
        scale = 0.02
        return {'hidden_states': jax.random.normal(ks[0], (B, HW, C), jnp.float32), 'encoder_hidden_states': jax.random.normal(ks[1], (B, T, CT), jnp.float32), 'mask_A': (jax.random.uniform(ks[2], (HW,)) > 0.5).astype(jnp.float32), 'mask_B': (jax.random.uniform(ks[3], (HW,)) > 0.5).astype(jnp.float32), 'Wq': jax.random.normal(ks[4], (C, inner), jnp.float32) * scale, 'Wk': jax.random.normal(ks[5], (CT, inner), jnp.float32) * scale, 'Wv': jax.random.normal(ks[6], (CT, inner), jnp.float32) * scale, 'Wo': jax.random.normal(ks[7], (inner, C), jnp.float32) * scale, 'bo': jnp.zeros((C,), jnp.float32), 'token_indices_A': jnp.array([2, 3], dtype=jnp.int64), 'token_indices_B': jnp.array([5, 6], dtype=jnp.int64)}
    _L0_xattn_all = _L0_xattn_setup()
    _L0_xattn_in = {k: v for k, v in _L0_xattn_all.items() if k in ('Wq', 'Wk', 'Wv', 'Wo', 'bo', 'token_indices_A', 'token_indices_B')}
    del _L0_xattn_all

    def _L1_xattn_setup():
        import jax, jax.numpy as jnp
        import numpy as np
        D_MODEL = 256
        N_HEADS = 16
        N_KV_HEADS = 4
        HEAD_DIM = D_MODEL // N_HEADS
        SPEAKER_DIM = 512
        EPS = 1e-05

        def rmsnorm(x, w, eps=EPS):
            xf = x.astype(jnp.float32)
            inv = jax.lax.rsqrt(jnp.mean(xf * xf, axis=-1, keepdims=True) + eps)
            return (xf * inv).astype(x.dtype) * w
        key = jax.random.key(seed)
        ks = jax.random.split(key, 7)
        B, T, S = (4, 512, 128)
        x = jax.random.normal(ks[0], (B, T, D_MODEL), dtype=jnp.float32)
        cond = jax.random.normal(ks[1], (B, S, SPEAKER_DIM), dtype=jnp.float32)
        sq = 0.02
        wq = jax.random.normal(ks[2], (D_MODEL, N_HEADS * HEAD_DIM), dtype=jnp.float32) * sq
        wk = jax.random.normal(ks[3], (SPEAKER_DIM, N_KV_HEADS * HEAD_DIM), dtype=jnp.float32) * sq
        wv = jax.random.normal(ks[4], (SPEAKER_DIM, N_KV_HEADS * HEAD_DIM), dtype=jnp.float32) * sq
        wo = jax.random.normal(ks[5], (N_HEADS * HEAD_DIM, D_MODEL), dtype=jnp.float32) * sq
        norm_w = jnp.ones((D_MODEL,), dtype=jnp.float32)
        return {'x': x, 'cond': cond, 'wq': wq, 'wk': wk, 'wv': wv, 'wo': wo, 'norm_w': norm_w}
    _L1_xattn_all = _L1_xattn_setup()
    _L1_xattn_in = {k: v for k, v in _L1_xattn_all.items() if k in ('wq', 'wk', 'wv', 'wo', 'norm_w')}
    del _L1_xattn_all

    def _L2_xattn_setup():
        import jax, jax.numpy as jnp
        import numpy as np
        HEADS = 16
        HEAD_DIM = 64
        SUPPRESS = 20.0
        key = jax.random.key(seed)
        ks = jax.random.split(key, 8)
        B, HW, C, T, CT = (8, 1024, 256, 77, 512)
        inner = HEADS * HEAD_DIM
        scale = 0.02
        return {'hidden_states': jax.random.normal(ks[0], (B, HW, C), jnp.float32), 'encoder_hidden_states': jax.random.normal(ks[1], (B, T, CT), jnp.float32), 'mask_A': (jax.random.uniform(ks[2], (HW,)) > 0.5).astype(jnp.float32), 'mask_B': (jax.random.uniform(ks[3], (HW,)) > 0.5).astype(jnp.float32), 'Wq': jax.random.normal(ks[4], (C, inner), jnp.float32) * scale, 'Wk': jax.random.normal(ks[5], (CT, inner), jnp.float32) * scale, 'Wv': jax.random.normal(ks[6], (CT, inner), jnp.float32) * scale, 'Wo': jax.random.normal(ks[7], (inner, C), jnp.float32) * scale, 'bo': jnp.zeros((C,), jnp.float32), 'token_indices_A': jnp.array([2, 3], dtype=jnp.int64), 'token_indices_B': jnp.array([5, 6], dtype=jnp.int64)}
    _L2_xattn_all = _L2_xattn_setup()
    _L2_xattn_in = {k: v for k, v in _L2_xattn_all.items() if k in ('Wq', 'Wk', 'Wv', 'Wo', 'bo', 'token_indices_A', 'token_indices_B')}
    del _L2_xattn_all

    def _L3_xattn_setup():
        import jax, jax.numpy as jnp
        import numpy as np
        HEADS = 16
        HEAD_DIM = 64
        SUPPRESS = 20.0
        key = jax.random.key(seed)
        ks = jax.random.split(key, 8)
        B, HW, C, T, CT = (8, 1024, 256, 77, 512)
        inner = HEADS * HEAD_DIM
        scale = 0.02
        return {'hidden_states': jax.random.normal(ks[0], (B, HW, C), jnp.float32), 'encoder_hidden_states': jax.random.normal(ks[1], (B, T, CT), jnp.float32), 'mask_A': (jax.random.uniform(ks[2], (HW,)) > 0.5).astype(jnp.float32), 'mask_B': (jax.random.uniform(ks[3], (HW,)) > 0.5).astype(jnp.float32), 'Wq': jax.random.normal(ks[4], (C, inner), jnp.float32) * scale, 'Wk': jax.random.normal(ks[5], (CT, inner), jnp.float32) * scale, 'Wv': jax.random.normal(ks[6], (CT, inner), jnp.float32) * scale, 'Wo': jax.random.normal(ks[7], (inner, C), jnp.float32) * scale, 'bo': jnp.zeros((C,), jnp.float32), 'token_indices_A': jnp.array([2, 3], dtype=jnp.int64), 'token_indices_B': jnp.array([5, 6], dtype=jnp.int64)}
    _L3_xattn_all = _L3_xattn_setup()
    _L3_xattn_in = {k: v for k, v in _L3_xattn_all.items() if k in ('Wq', 'Wk', 'Wv', 'Wo', 'bo', 'token_indices_A', 'token_indices_B')}
    del _L3_xattn_all
    return {'x': x, 'ctx_2048': ctx_2048, 'mask_S_fk1': mask_S_fk1, 'mask_S_fk0': mask_S_fk0, 'L0_xattn_Wq': _L0_xattn_in['Wq'], 'L0_xattn_Wk': _L0_xattn_in['Wk'], 'L0_xattn_Wv': _L0_xattn_in['Wv'], 'L0_xattn_Wo': _L0_xattn_in['Wo'], 'L0_xattn_bo': _L0_xattn_in['bo'], 'L0_xattn_token_indices_A': _L0_xattn_in['token_indices_A'], 'L0_xattn_token_indices_B': _L0_xattn_in['token_indices_B'], 'L1_xattn_wq': _L1_xattn_in['wq'], 'L1_xattn_wk': _L1_xattn_in['wk'], 'L1_xattn_wv': _L1_xattn_in['wv'], 'L1_xattn_wo': _L1_xattn_in['wo'], 'L1_xattn_norm_w': _L1_xattn_in['norm_w'], 'L2_xattn_Wq': _L2_xattn_in['Wq'], 'L2_xattn_Wk': _L2_xattn_in['Wk'], 'L2_xattn_Wv': _L2_xattn_in['Wv'], 'L2_xattn_Wo': _L2_xattn_in['Wo'], 'L2_xattn_bo': _L2_xattn_in['bo'], 'L2_xattn_token_indices_A': _L2_xattn_in['token_indices_A'], 'L2_xattn_token_indices_B': _L2_xattn_in['token_indices_B'], 'L3_xattn_Wq': _L3_xattn_in['Wq'], 'L3_xattn_Wk': _L3_xattn_in['Wk'], 'L3_xattn_Wv': _L3_xattn_in['Wv'], 'L3_xattn_Wo': _L3_xattn_in['Wo'], 'L3_xattn_bo': _L3_xattn_in['bo'], 'L3_xattn_token_indices_A': _L3_xattn_in['token_indices_A'], 'L3_xattn_token_indices_B': _L3_xattn_in['token_indices_B']}

def reference(x, ctx_2048, mask_S_fk1, mask_S_fk0, L0_xattn_Wq, L0_xattn_Wk, L0_xattn_Wv, L0_xattn_Wo, L0_xattn_bo, L0_xattn_token_indices_A, L0_xattn_token_indices_B, L1_xattn_wq, L1_xattn_wk, L1_xattn_wv, L1_xattn_wo, L1_xattn_norm_w, L2_xattn_Wq, L2_xattn_Wk, L2_xattn_Wv, L2_xattn_Wo, L2_xattn_bo, L2_xattn_token_indices_A, L2_xattn_token_indices_B, L3_xattn_Wq, L3_xattn_Wk, L3_xattn_Wv, L3_xattn_Wo, L3_xattn_bo, L3_xattn_token_indices_A, L3_xattn_token_indices_B):
    import jax
    import jax.numpy as jnp

    def _L0_xattn_ref(hidden_states, encoder_hidden_states, mask_A, mask_B, Wq, Wk, Wv, Wo, bo, token_indices_A, token_indices_B):
        import jax, jax.numpy as jnp
        import numpy as np
        HEADS = 16
        HEAD_DIM = 64
        SUPPRESS = 20.0
        B, HW, C = hidden_states.shape
        T = encoder_hidden_states.shape[1]
        residual = hidden_states
        q = hidden_states @ Wq
        k = encoder_hidden_states @ Wk
        v = encoder_hidden_states @ Wv
        q = q.reshape(B, HW, HEADS, HEAD_DIM).transpose(0, 2, 1, 3)
        k = k.reshape(B, T, HEADS, HEAD_DIM).transpose(0, 2, 1, 3)
        v = v.reshape(B, T, HEADS, HEAD_DIM).transpose(0, 2, 1, 3)
        scale = HEAD_DIM ** (-0.5)
        logits = jnp.einsum('bhqd,bhkd->bhqk', q, k) * scale
        suppress_A_in = 1.0 - mask_A
        suppress_B_in = 1.0 - mask_B
        col_bias = jnp.zeros((HW, T), logits.dtype)
        col_bias = col_bias.at[:, token_indices_A].set((-SUPPRESS * suppress_A_in)[:, None])
        col_bias = col_bias.at[:, token_indices_B].set((-SUPPRESS * suppress_B_in)[:, None])
        logits = logits + col_bias[None, None, :, :]
        probs = jax.nn.softmax(logits, axis=-1)
        out = jnp.einsum('bhqk,bhkd->bhqd', probs, v)
        out = out.transpose(0, 2, 1, 3).reshape(B, HW, HEADS * HEAD_DIM)
        out = out @ Wo + bo
        out = out + residual
        return out

    def _L1_xattn_ref(x, cond, wq, wk, wv, wo, norm_w):
        import jax, jax.numpy as jnp
        import numpy as np
        D_MODEL = 256
        N_HEADS = 16
        N_KV_HEADS = 4
        HEAD_DIM = D_MODEL // N_HEADS
        SPEAKER_DIM = 512
        EPS = 1e-05

        def rmsnorm(x, w, eps=EPS):
            xf = x.astype(jnp.float32)
            inv = jax.lax.rsqrt(jnp.mean(xf * xf, axis=-1, keepdims=True) + eps)
            return (xf * inv).astype(x.dtype) * w
        B, T, _ = x.shape
        S = cond.shape[1]
        n_rep = N_HEADS // N_KV_HEADS
        residual = x
        xn = rmsnorm(x, norm_w)
        q = (xn @ wq).reshape(B, T, N_HEADS, HEAD_DIM)
        k = (cond @ wk).reshape(B, S, N_KV_HEADS, HEAD_DIM)
        v = (cond @ wv).reshape(B, S, N_KV_HEADS, HEAD_DIM)
        qg = q.reshape(B, T, N_KV_HEADS, n_rep, HEAD_DIM)
        scale = 1.0 / np.sqrt(HEAD_DIM).astype(np.float32)
        scores = jnp.einsum('btgrd,bsgd->bgrts', qg, k) * scale
        attn = jax.nn.softmax(scores.astype(jnp.float32), axis=-1).astype(q.dtype)
        out = jnp.einsum('bgrts,bsgd->btgrd', attn, v).reshape(B, T, N_HEADS * HEAD_DIM)
        return residual + out @ wo

    def _L2_xattn_ref(hidden_states, encoder_hidden_states, mask_A, mask_B, Wq, Wk, Wv, Wo, bo, token_indices_A, token_indices_B):
        import jax, jax.numpy as jnp
        import numpy as np
        HEADS = 16
        HEAD_DIM = 64
        SUPPRESS = 20.0
        B, HW, C = hidden_states.shape
        T = encoder_hidden_states.shape[1]
        residual = hidden_states
        q = hidden_states @ Wq
        k = encoder_hidden_states @ Wk
        v = encoder_hidden_states @ Wv
        q = q.reshape(B, HW, HEADS, HEAD_DIM).transpose(0, 2, 1, 3)
        k = k.reshape(B, T, HEADS, HEAD_DIM).transpose(0, 2, 1, 3)
        v = v.reshape(B, T, HEADS, HEAD_DIM).transpose(0, 2, 1, 3)
        scale = HEAD_DIM ** (-0.5)
        logits = jnp.einsum('bhqd,bhkd->bhqk', q, k) * scale
        suppress_A_in = 1.0 - mask_A
        suppress_B_in = 1.0 - mask_B
        col_bias = jnp.zeros((HW, T), logits.dtype)
        col_bias = col_bias.at[:, token_indices_A].set((-SUPPRESS * suppress_A_in)[:, None])
        col_bias = col_bias.at[:, token_indices_B].set((-SUPPRESS * suppress_B_in)[:, None])
        logits = logits + col_bias[None, None, :, :]
        probs = jax.nn.softmax(logits, axis=-1)
        out = jnp.einsum('bhqk,bhkd->bhqd', probs, v)
        out = out.transpose(0, 2, 1, 3).reshape(B, HW, HEADS * HEAD_DIM)
        out = out @ Wo + bo
        out = out + residual
        return out

    def _L3_xattn_ref(hidden_states, encoder_hidden_states, mask_A, mask_B, Wq, Wk, Wv, Wo, bo, token_indices_A, token_indices_B):
        import jax, jax.numpy as jnp
        import numpy as np
        HEADS = 16
        HEAD_DIM = 64
        SUPPRESS = 20.0
        B, HW, C = hidden_states.shape
        T = encoder_hidden_states.shape[1]
        residual = hidden_states
        q = hidden_states @ Wq
        k = encoder_hidden_states @ Wk
        v = encoder_hidden_states @ Wv
        q = q.reshape(B, HW, HEADS, HEAD_DIM).transpose(0, 2, 1, 3)
        k = k.reshape(B, T, HEADS, HEAD_DIM).transpose(0, 2, 1, 3)
        v = v.reshape(B, T, HEADS, HEAD_DIM).transpose(0, 2, 1, 3)
        scale = HEAD_DIM ** (-0.5)
        logits = jnp.einsum('bhqd,bhkd->bhqk', q, k) * scale
        suppress_A_in = 1.0 - mask_A
        suppress_B_in = 1.0 - mask_B
        col_bias = jnp.zeros((HW, T), logits.dtype)
        col_bias = col_bias.at[:, token_indices_A].set((-SUPPRESS * suppress_A_in)[:, None])
        col_bias = col_bias.at[:, token_indices_B].set((-SUPPRESS * suppress_B_in)[:, None])
        logits = logits + col_bias[None, None, :, :]
        probs = jax.nn.softmax(logits, axis=-1)
        out = jnp.einsum('bhqk,bhkd->bhqd', probs, v)
        out = out.transpose(0, 2, 1, 3).reshape(B, HW, HEADS * HEAD_DIM)
        out = out @ Wo + bo
        out = out + residual
        return out
    x = _L0_xattn_ref(x, ctx_2048, mask_S_fk1, mask_S_fk0, L0_xattn_Wq, L0_xattn_Wk, L0_xattn_Wv, L0_xattn_Wo, L0_xattn_bo, L0_xattn_token_indices_A, L0_xattn_token_indices_B)
    x = _L1_xattn_ref(x, ctx_2048, L1_xattn_wq, L1_xattn_wk, L1_xattn_wv, L1_xattn_wo, L1_xattn_norm_w)
    x = _L2_xattn_ref(x, ctx_2048, mask_S_fk1, mask_S_fk0, L2_xattn_Wq, L2_xattn_Wk, L2_xattn_Wv, L2_xattn_Wo, L2_xattn_bo, L2_xattn_token_indices_A, L2_xattn_token_indices_B)
    x = _L3_xattn_ref(x, ctx_2048, mask_S_fk1, mask_S_fk0, L3_xattn_Wq, L3_xattn_Wk, L3_xattn_Wv, L3_xattn_Wo, L3_xattn_bo, L3_xattn_token_indices_A, L3_xattn_token_indices_B)
    return x

_drawn_inputs = setup_inputs


def setup_inputs(seed=0):
    import zlib

    import numpy as np

    out = dict(_drawn_inputs(seed))
    spreads = {'L0_xattn_bo': (0.0, 0.1),
     'L1_xattn_norm_w': (1.0, 0.6),
     'L2_xattn_bo': (0.0, 0.1),
     'L3_xattn_bo': (0.0, 0.1)}
    factors = {'mask_S_fk1': 8.0,
     'mask_S_fk0': 8.0,
     'L0_xattn_Wq': 8.0,
     'L0_xattn_Wk': 8.0,
     'L1_xattn_wq': 8.0,
     'L1_xattn_wk': 8.0,
     'L2_xattn_Wq': 8.0,
     'L2_xattn_Wk': 8.0,
     'L3_xattn_Wq': 8.0,
     'L3_xattn_Wk': 8.0}
    for name, (base, spread) in spreads.items():
        noise = np.random.default_rng([zlib.crc32(name.encode()), seed]).standard_normal(out[name].shape)
        drawn = base * np.exp(spread * noise) if base else spread * noise
        out[name] = jnp.asarray(drawn.astype(out[name].dtype))
    for name, factor in factors.items():
        out[name] = (out[name] * factor).astype(out[name].dtype)
    return out
```

```python
from contextlib import ExitStack

import numpy as np
import concourse.bass as bass
from concourse import mybir
from concourse.alu_op_type import AluOpType as ALU

F32 = mybir.dt.float32
F32R = mybir.dt.float32r
I32 = mybir.dt.int32
ACT = mybir.ActivationFunctionType
AX = mybir.AxisListType

P128 = 128
LAYERS, HEADS, D = 4, 16, 64
NQ, NK, C, CC = 2048, 1601, 256, 512
PAIRS = HEADS // 2
QT, KT = NQ // P128, -(-NK // P128)
KREST = NK - (KT - 1) * P128
KP = NK + 1
KCH = [(0, 402), (402, 400), (802, 400), (1202, 400)]
JQ = NQ // 512
CT, CCT = C // P128, CC // P128
NP = 6
STEPS = 2 * KT
UNITS = 2 * STEPS
SUNITS = QT * len(KCH)
SUPPRESS, SCALE, EPS = 20.0, 0.125, 1e-5
NROWS = 5
NONE = 4096


def s_units(step):
    first, steps = 2, STEPS - 2
    if step < first:
        return range(0)
    a, b = step - first, step - first + 1
    return range(a * SUNITS // steps, b * SUNITS // steps)


def words(ap):
    return ap.bitcast(F32)


def rows_of(t):
    return KREST if t == KT - 1 else P128


class Pair:

    def __init__(self, eng, n, start, ahead=()):
        self.eng, self.n, self.start, self.made = eng, n, start, {}
        self.ahead = {(m, c): eng.snap(n * m + c) for m, c in ahead}

    def wait(self, sem, per_pair, plus):
        plus += self.start.get(sem.name, 0)
        if (per_pair, plus) in self.ahead:
            self.eng.wait_ge(sem, self.ahead[per_pair, plus])
            return
        if per_pair not in self.made:
            self.made[per_pair] = self.eng.snap(self.n * per_pair)
        self.eng.wait_ge(sem, self.made[per_pair] + plus)


def attention_layers(nc, a):
    with ExitStack() as ctx:
        def sb(name, shape, dt=F32):
            return ctx.enter_context(nc.sbuf_tensor(name, shape, dt))

        start = {}

        def sem(name):
            return ctx.enter_context(nc.semaphore(name))

        def from_one(name):
            start[name] = 1
            return sem(name)

        ctxT = sb("ctxT", [128, CCT, KP])
        xacc = sb("xacc", [128, CT, NQ])
        xq = sb("xq", [128, CT, NQ])
        ident = sb("ident", [128, 128])
        ones = sb("ones", [128, 128])
        wk = sb("wk", [128, CCT, 128])
        wv = sb("wv", [128, CCT, 128])
        wq = sb("wq", [128, CT, 128])
        wo = sb("wo", [128, C])
        rawK = sb("rawK", [128, KP])
        rawQ = sb("rawQ", [128, NQ])
        rawV = sb("rawV", [128, NK])
        V = sb("V", [128, KT, 128])
        Q1 = [sb(f"Q1_{b}", [128, NQ], F32R) for b in range(2)]
        Q2 = [sb(f"Q2_{b}", [128, NQ], F32R) for b in range(2)]
        K1 = [sb(f"K1_{b}", [128, KP], F32R) for b in range(2)]
        K2 = [sb(f"K2_{b}", [128, KP], F32R) for b in range(2)]
        KS = [sb(f"KS_{b}", [128, KP], F32R) for b in range(2)]
        P = sb("P", [128, NP, 512])
        acc = sb("acc", [128, 2, 2, 512])
        Oraw = sb("Oraw", [128, 2, 512])
        R = sb("R", [128, 512])
        On = sb("On", [128, NQ])
        mpart = sb("mpart", [128, QT, len(KCH)])
        negm = sb("negm", [128, QT])
        mrow = sb("mrow", [QT, 128], F32R)
        tok_i = sb("tok_i", [NROWS, 4], I32)
        tok = sb("tok", [NROWS, 8])
        first_row = sb("first_row", [NROWS, 1])
        nw = sb("nw", [128, CT])
        bo = sb("bo", [128, CT])
        ab = sb("ab", [128, 2])

        ST = [ctx.enter_context(nc.psum_tensor(f"ST{i}", [128, 512], F32)) for i in range(4)]
        SS = [ctx.enter_context(nc.psum_tensor(f"SS{i}", [128, 512], F32)) for i in range(2)]
        OB = ctx.enter_context(nc.psum_tensor("OB", [128, 512], F32))
        ZB = ctx.enter_context(nc.psum_tensor("ZB", [128, 512], F32))

        d_in = sem("d_in")
        d_biasrow = sem("d_biasrow")
        d_layer = sem("d_layer")
        d_ext = sem("d_ext")
        d_out = sem("d_out")
        pool_set = sem("pool_set")
        pe_set = sem("pe_set")
        act_set = sem("act_set")
        dve_set = sem("dve_set")
        dve_zero = sem("dve_zero")
        dve_bias = sem("dve_bias")
        dve_tok = sem("dve_tok")
        dve_ext = sem("dve_ext")
        act_sq = sem("act_sq")
        pe_sq = sem("pe_sq")
        dve_var = sem("dve_var")
        act_rms = sem("act_rms")
        dve_xq = sem("dve_xq")
        dve_bo = sem("dve_bo")
        dve_own = sem("dve_own")
        pe_out = sem("pe_out")
        dve_out = sem("dve_out")
        d_wkq, d_wv, d_wo = sem("d_wkq"), sem("d_wv"), sem("d_wo")
        pe_kq = sem("pe_kq")
        act_kq = sem("act_kq")
        pe_v = sem("pe_v")
        act_vraw = sem("act_vraw")
        pe_vt = sem("pe_vt")
        act_v = sem("act_v")
        pe_o = from_one("pe_o")
        dve_x = from_one("dve_x")
        act_hi = sem("act_hi")
        dve_lo = sem("dve_lo")
        pe_s = sem("pe_s")
        dve_s = from_one("dve_s")
        dve_m = from_one("dve_m")
        pe_m = sem("pe_m")
        dve_mrow = from_one("dve_mrow")
        d_m = sem("d_m")
        pe_st = from_one("pe_st")
        act_p = sem("act_p")
        pool_acc = from_one("pool_acc")
        pe_pv = from_one("pe_pv")
        act_o = from_one("act_o")
        pe_z = from_one("pe_z")
        dve_r = from_one("dve_r")
        dve_on = from_one("dve_on")

        start["d_m"] = 16

        block = ctx.enter_context(nc.Block())

        x_land = [rawQ[:, :].rearrange("p (t c) -> p t c", c=C), On[:, :].rearrange("p (t c) -> p t c", c=C)]
        ctx_land = [P[:, i, :] for i in range(6)] + [acc[:, i // 2, i % 2, :] for i in range(4)] \
            + [Oraw[:, i, :] for i in range(2)] + [R[0:KREST, :]]
        XH = QT // 2
        x_out = xq[:, :, :].rearrange("p a b -> p (a b)").rearrange("p (t c) -> p t c", c=C)

        @block.sync
        def _(sp):
            for i in range(2):
                sp.dma_start(x_land[i], a["x"][i * XH * 128:(i + 1) * XH * 128, :]
                             .rearrange("(t p) c -> p t c", p=128)).then_inc(d_in, 16)
            sp.dma_start(P[:, :, :], a["ctx"][0:768, :].rearrange("(t p) c -> p t c", p=128)).then_inc(d_in, 16)
            sp.dma_start(acc[:, :, :, :].rearrange("p a b c -> p (a b) c"),
                         a["ctx"][768:1280, :].rearrange("(t p) c -> p t c", p=128)).then_inc(d_in, 16)
            sp.dma_start(Oraw[:, :, :], a["ctx"][1280:1536, :].rearrange("(t p) c -> p t c", p=128)).then_inc(d_in, 16)
            sp.dma_start(R[0:KREST, :], a["ctx"][1536:NK, :]).then_inc(d_in, 16)
            sp.dma_start(xq[0:2, 0, :], a["mask"][:, :]).then_inc(d_m, 16)
            sp.dma_start(wk[:, :, :], a["wk"][0, :, :, :]).then_inc(d_wkq, 16)
            sp.dma_start(wq[:, :, :], a["wq"][0, :, :, :]).then_inc(d_wkq, 16)
            sp.dma_start(wv[:, :, :], a["wv"][0, :, :, :]).then_inc(d_wv, 16)
            sp.dma_start(wo[:, :], a["wo"][0, :, :]).then_inc(d_wo, 16)
            sp.wait_ge(dve_bias, 3)
            sp.wait_ge(dve_zero, 6)
            for b in range(2):
                o = 64 * (1 - b)
                for r in range(4):
                    sp.dma_start(words(Q2[b][o + 1 + r:o + 2 + r, :]), words(Q1[r % 2][r // 2:r // 2 + 1, :])).then_inc(d_biasrow, 16)
            sp.wait_ge(d_biasrow, 128)

            def load_kq(n):
                sp.dma_start(wk[:, :, :], a["wk"][n, :, :, :]).then_inc(d_wkq, 16)
                sp.dma_start(wq[:, :, :], a["wq"][n, :, :, :]).then_inc(d_wkq, 16)

            def max_row(b, pr, g):
                pr.wait(dve_mrow, 2, g + 1)
                o = 64 * (1 - b)
                sp.dma_start(words(Q2[b][o:o + 1, :]).rearrange("o (t p) -> o t p", p=128), words(mrow[:, :])).then_inc(d_m, 16)

            def pair(l, p, last):
                n = sp.snap(l * PAIRS + p)
                n1, n2 = sp.snap(n + 1), sp.snap(n + 2)
                pr = Pair(sp, n, start, [(2, 3), (8, 9)] + ([] if last else [(8, 16), (2, 4), (4, 8)]))
                max_row(1, pr, 1)
                if not last:
                    pr.wait(pe_kq, 8, 16)
                    load_kq(n2)
                    max_row(0, pr, 2)
                    pr.wait(pe_v, 4, 8)
                    sp.dma_start(wv[:, :, :], a["wv"][n2, :, :, :]).then_inc(d_wv, 16)
                pr.wait(pe_o, 8, 8)
                sp.dma_start(wo[:, :], a["wo"][n1, :, :]).then_inc(d_wo, 16)

            with sp.Fori(0, LAYERS) as l:
                n0 = sp.snap(l * PAIRS)
                n1 = sp.snap(n0 + 1)
                l1, written = sp.snap(l + 1), sp.snap(l * (8 * PAIRS) + 1)
                pr = Pair(sp, n0, start, [(8, 8), (4, 4), (2, 2)])
                sp.wait_ge(pe_o, written)
                sp.dma_start(rawK[0:NROWS, :], a["key"][:, :]).then_inc(d_layer, 16)
                sp.dma_start(tok_i[:, :], a["tok"][l, :, :]).then_inc(d_layer, 16)
                sp.dma_start(nw[:, :], a["nw"][l, :, :]).then_inc(d_layer, 16)
                sp.dma_start(bo[:, :], a["bo"][l, :, :]).then_inc(d_layer, 16)
                sp.dma_start(ab[:, :], a["ab"][l, :, :]).then_inc(d_layer, 16)
                sp.wait_ge(dve_ext, l1)
                for b in range(2):
                    o = 64 * (1 - b)
                    sp.dma_start(words(K2[b][o:o + NROWS, :]), words(K1[1][0:NROWS, :])).then_inc(d_ext, 16)
                    sp.dma_start(words(KS[b][o + 1:o + NROWS, :]), words(K1[1][1:NROWS, :])).then_inc(d_ext, 16)
                pr.wait(pe_kq, 8, 8)
                load_kq(n1)
                pr.wait(pe_v, 4, 4)
                sp.dma_start(wv[:, :, :], a["wv"][n1, :, :, :]).then_inc(d_wv, 16)
                max_row(0, pr, 0)
                with sp.Fori(0, PAIRS - 1) as p:
                    pair(l, p, False)
                pair(l, PAIRS - 1, True)

            for t in range(0, QT, 4):
                sp.wait_ge(dve_out, t + 4)
                sp.dma_start(a["out"][t * 128:(t + 4) * 128, :].rearrange("(t p) c -> p t c", p=128),
                             x_out[:, t:t + 4, :]).then_inc(d_out, 16)
            sp.wait_ge(d_out, 16 * QT // 4)
            sp.wait_ge(d_wkq, 32 * (LAYERS * PAIRS + 1))
            sp.wait_ge(d_wv, 16 * (LAYERS * PAIRS + 1))
            sp.wait_ge(d_wo, 16 * (LAYERS * PAIRS + 1))

        @block.gpsimd
        def _(gp):
            gp.sem_inc(pool_acc, 1)
            gp.memset(ident[:, :], 0.0).then_inc(pool_set, 1)
            gp.wait_ge(pool_set, 1)
            gp.affine_select(out=ident[:, :], in_=ident[:, :], compare_op=ALU.not_equal, fill=1.0, base=0,
                             pattern=[[-1, 128]], channel_multiplier=1).then_inc(pool_set, 1)
            gp.memset(ones[:, :], 1.0).then_inc(pool_set, 1)
            gp.wait_ge(pool_set, 3)
            gp.iota(tok[:, 7:8].bitcast(I32), [[0, 1]], base=0, channel_multiplier=1).then_inc(pool_set, 1)

            def head(pr, g):
                for u in range(UNITS):
                    c2, t, jj = u // (2 * KT), u // 2 % KT, u % 2
                    if t == 0:
                        continue
                    k = rows_of(t)
                    out = acc[0:k, c2, jj, :]
                    pr.wait(act_p, 2 * UNITS, g * UNITS + u + 1)
                    if t == 1:
                        pr.wait(pe_z, 4, 2 * g)
                        gp.tensor_tensor(out, P[:, (u - 2) % NP, :], P[:, u % NP, :], ALU.add)\
                            .then_inc(pool_acc, 1 + 2 * jj)
                    else:
                        pr.wait(pool_acc, 2 * UNITS, g * UNITS + u - 1)
                        gp.tensor_tensor(out, out, P[0:k, u % NP, :], ALU.add).then_inc(pool_acc, 1)

            with gp.Fori(0, LAYERS * PAIRS) as n:
                pr = Pair(gp, n, start)
                for g in range(2):
                    head(pr, g)

        @block.tensor
        def _(pe):
            for s in (pe_z, pe_pv, pe_o, pe_st):
                pe.sem_inc(s, 1)
            pe.wait_ge(pool_set, 3)
            pe.wait_ge(d_in, 96)
            for i in range(QT // 2):
                if i >= 4:
                    pe.wait_ge(act_set, i - 3)
                for k in range(4):
                    t, ct = 2 * i + k // 2, k % 2
                    last = pe.transpose(ST[i % 4][:, k * 128:(k + 1) * 128],
                                        x_land[t // XH][:, t % XH, ct * 128:(ct + 1) * 128], ident[:, :])
                last.then_inc(pe_set, 1)
            for t in range(KT):
                i = QT // 2 + t
                pe.wait_ge(act_set, i - 3)
                k = rows_of(t)
                for ct in range(CCT):
                    last = pe.transpose(ST[i % 4][:, ct * 128:ct * 128 + k],
                                        ctx_land[t][0:k, ct * 128:(ct + 1) * 128], ident[0:k, 0:k])
                last.then_inc(pe_set, 1)
            NSET = QT // 2 + KT

            def project_kq(pr, n, first_waits):
                pr.wait(d_wkq, 32, 32 * (n + 1))
                for i in range(8):
                    if i < 4:
                        if i == 0:
                            first_waits()
                    else:
                        pr.wait(act_kq, 8, 8 * n + i - 3)
                    b = ST[i % 4]
                    if i < 4:
                        o, w = KCH[i]
                        for ct in range(CCT):
                            last = pe.matmul(b[:, 0:w], wk[:, ct, :], ctxT[:, ct, o:o + w],
                                             start=ct == 0, stop=ct == CCT - 1)
                    else:
                        j = i - 4
                        for ct in range(CT):
                            last = pe.matmul(b[:, :], wq[:, ct, :], xq[:, ct, j * 512:(j + 1) * 512],
                                             start=ct == 0, stop=ct == CT - 1)
                    last.then_inc(pe_kq, 1)
                    if i == 3:
                        yield

            def project_v(pr, n, first_waits):
                pr.wait(d_wv, 16, 16 * (n + 1))
                for i, (o, w) in enumerate(KCH):
                    first_waits(i)
                    w = min(w, NK - o)
                    for ct in range(CCT):
                        last = pe.matmul(ST[i][:, 0:w], wv[:, ct, :], ctxT[:, ct, o:o + w],
                                         start=ct == 0, stop=ct == CCT - 1)
                    last.then_inc(pe_v, 1)

            def transpose_v(pr, n):
                pr.wait(act_vraw, 4, 4 * (n + 1))
                for i in range(4):
                    for t in range(4 * i, min(4 * i + 4, KT)):
                        k, c = rows_of(t), t - 4 * i
                        last = pe.transpose(ST[i][0:k, c * 128:(c + 1) * 128], rawV[:, t * 128:t * 128 + k], ident[:, :])
                    last.then_inc(pe_vt, 1)

            def s_tile(pr, g, i):
                b = g % 2
                if i == 0:
                    pr.wait(act_hi, 10, 5 * (g + 1))
                    pr.wait(dve_mrow, 2, g)
                    pr.wait(dve_s, 2 * SUNITS, g * SUNITS)
                if i >= 2:
                    pr.wait(dve_s, 2 * SUNITS, g * SUNITS + i - 1)
                qt, (o, w) = i // len(KCH), KCH[i % len(KCH)]
                pe.matmul(SS[i % 2][:, 0:w], Q2[b][:, qt * 128:(qt + 1) * 128], KS[b][:, o:o + w],
                          start=True, stop=True).then_inc(pe_s, 1)

            def transpose_max(pr, g):
                pr.wait(dve_m, 2, g + 1)
                pe.transpose(SS[0][0:QT, 0:128], negm[:, :], ident[:, :]).then_inc(pe_m, 1)

            def sums(pr, g, c2):
                pr.wait(pool_acc, 2 * UNITS, g * UNITS + (c2 + 1) * 2 * KT)
                pr.wait(dve_r, 4, 2 * g + c2)
                for jj in range(2):
                    last = pe.matmul(ZB[64 * jj:64 * jj + 64, :], ones[:, 0:64], acc[:, c2, jj, :],
                                     start=True, stop=True)
                last.then_inc(pe_z, 1)

            def attend(pr, g, first_waits, other):
                b = g % 2

                def scores(s, jj):
                    c2, t = s // KT, s % KT
                    k, u, j = rows_of(t), 2 * s + jj, 2 * c2 + jj
                    if u >= 4:
                        pr.wait(act_p, 2 * UNITS, g * UNITS + u - 3)
                    bank = ST[u % 4][0:k, :]
                    pe.matmul(bank, K1[b][:, t * 128:t * 128 + k], Q1[b][:, j * 512:(j + 1) * 512],
                              start=True, stop=False)
                    pe.matmul(bank, K2[b][:, t * 128:t * 128 + k], Q2[b][:, j * 512:(j + 1) * 512],
                              start=False, stop=True).then_inc(pe_st, 1)

                def s_next(tiles, last=False):
                    for i in tiles if last else tiles[:1]:
                        s_tile(pr, other, i)
                    return tiles[1:]

                first_waits()
                pr.wait(act_hi, 10, 5 * (g + 1))
                pr.wait(dve_lo, 4, 2 * (g + 1))
                pr.wait(d_m, 32, 16 * (g + 1))
                for jj in range(2):
                    scores(0, jj)
                for s in range(STEPS):
                    c2, t = s // KT, s % KT
                    k = rows_of(t)
                    tiles = [] if other is None else list(s_units(s))
                    for jj in range(2):
                        if s + 1 < STEPS:
                            scores(s + 1, jj)
                        tiles = s_next(tiles)
                    pr.wait(act_p, 2 * UNITS, g * UNITS + 2 * s + 2)
                    if t == 0:
                        pr.wait(act_o, 4, 2 * g + c2)
                    for jj in range(2):
                        last = pe.matmul(OB[64 * jj:64 * jj + 64, :], V[0:k, t, 64 * b:64 * b + 64],
                                         P[0:k, (2 * s + jj) % NP, :], start=t == 0, stop=t == KT - 1)
                    last.then_inc(pe_pv, 1)
                    s_next(tiles, last=True)
                    if s == KT + 3:
                        sums(pr, g, 0)

            def output(pr, first_waits):
                pr.wait(d_wo, 16, 16)
                pr.wait(dve_on, 8, 8)
                for i in range(CT * JQ):
                    ct, j = i // JQ, i % JQ
                    if i == 0:
                        first_waits()
                    if i >= 4:
                        pr.wait(dve_x, 8, i - 3)
                    pe.matmul(ST[i % 4][:, :], wo[:, ct * 128:(ct + 1) * 128], On[:, j * 512:(j + 1) * 512],
                              start=True, stop=True).then_inc(pe_o, 1)

            def pair(l, p, last):
                pr = Pair(pe, pe.snap(l * PAIRS + p), start)

                def before_a():
                    pr.wait(dve_x, 8, 0)
                    pr.wait(act_v, 4, 4)
                attend(pr, 0, before_a, 1)
                if last:
                    transpose_max(pr, 1)
                    sums(pr, 0, 1)
                else:
                    kq = project_kq(pr, 1, lambda: pr.wait(act_p, 2 * UNITS, UNITS))
                    next(kq)
                    transpose_max(pr, 1)
                    sums(pr, 0, 1)
                    for _ in kq:
                        pass
                attend(pr, 1, lambda: pr.wait(act_kq, 8, 8 if last else 16), None if last else 2)
                if last:
                    sums(pr, 1, 1)
                    output(pr, lambda: pr.wait(act_p, 2 * UNITS, 2 * UNITS))
                else:
                    project_v(pr, 1, lambda i: pr.wait(act_p, 2 * UNITS, 2 * UNITS) if i == 0 else None)
                    transpose_max(pr, 2)
                    sums(pr, 1, 1)
                    transpose_v(pr, 1)
                    output(pr, lambda: pr.wait(act_v, 4, 8))

            with pe.Fori(0, LAYERS) as l:
                pe.wait_ge(act_set, NSET)
                pe.wait_ge(dve_x, l * (8 * PAIRS) + 1)
                for j in range(JQ):
                    pe.wait_ge(act_sq, l * JQ + (j + 1))
                    for ct in range(CT):
                        last = pe.matmul(ST[j][:, :], ones[:, :], P[:, 2 * (j % 2) + ct, :],
                                         start=ct == 0, stop=ct == CT - 1)
                    last.then_inc(pe_sq, 1)
                pr = Pair(pe, pe.snap(l * PAIRS), start)
                pe.wait_ge(dve_var, l * JQ + JQ)
                kq = project_kq(pr, 0, lambda: None)
                next(kq)
                pe.wait_ge(dve_xq, l + 1)
                for _ in kq:
                    pass
                project_v(pr, 0, lambda i: pr.wait(act_kq, 8, 5 + i))
                transpose_v(pr, 0)
                pe.wait_ge(d_ext, l * 64 + 64)
                for i in range(SUNITS):
                    s_tile(pr, 0, i)
                transpose_max(pr, 0)
                with pe.Fori(0, PAIRS - 1) as p:
                    pair(l, p, False)
                pair(l, PAIRS - 1, True)

            pe.wait_ge(dve_x, LAYERS * PAIRS * 8 + 1)
            for t in range(QT):
                if t >= 4:
                    pe.wait_ge(dve_out, t - 3)
                for ct in range(CT):
                    last = pe.transpose(ST[t % 4][:, ct * 128:(ct + 1) * 128], xacc[:, ct, t * 128:(t + 1) * 128],
                                        ident[:, :])
                last.then_inc(pe_out, 1)

        @block.scalar
        def _(act):
            act.sem_inc(act_o, 1)

            def copy(out, in_):
                return act.activation(out, in_, ACT.Copy)

            for i in range(QT // 2):
                act.wait_ge(pe_set, i + 1)
                copy(xacc[:, :, 2 * i * 128:(2 * i + 2) * 128].rearrange("p c (t q) -> p c t q", t=2),
                     ST[i % 4][:, :].rearrange("p (t c q) -> p c t q", t=2, c=2)).then_inc(act_set, 1)
            for t in range(KT):
                i = QT // 2 + t
                k = rows_of(t)
                act.wait_ge(pe_set, i + 1)
                copy(ctxT[:, :, t * 128:t * 128 + k],
                     ST[i % 4][:, :].rearrange("p (c k) -> p c k", c=CCT)[:, :, 0:k]).then_inc(act_set, 1)
            copy(ctxT[:, :, NK:KP], ST[(QT // 2 + KT - 1) % 4][:, :].rearrange("p (c k) -> p c k", c=CCT)
                 [:, :, KREST - 1:KREST]).then_inc(act_set, 1)

            def raw_kq(pr, n, which):
                for i in which:
                    pr.wait(pe_kq, 8, 8 * n + i + 1)
                    if i < 4:
                        o, w = KCH[i]
                        copy(rawK[:, o:o + w], ST[i % 4][:, 0:w]).then_inc(act_kq, 1)
                    else:
                        copy(rawQ[:, (i - 4) * 512:(i - 3) * 512], ST[i % 4][:, :]).then_inc(act_kq, 1)

            def hi_k(pr, n, g):
                b = g % 2
                own, other = slice(64 * b, 64 * b + 64), slice(64 * (1 - b), 64 * (1 - b) + 64)
                pr.wait(act_kq, 8, 8 * n + 4)
                for out in (K1[b][own, :], K1[b][other, :], KS[b][own, :]):
                    copy(out, rawK[own, :]).then_inc(act_hi, 1)

            def hi_q(pr, n, g):
                b = g % 2
                own = slice(64 * b, 64 * b + 64)
                pr.wait(act_kq, 8, 8 * n + 8)
                for out in (Q1[b][own, :], Q2[b][own, :]):
                    copy(out, rawQ[own, :]).then_inc(act_hi, 1)

            def raw_v(pr, n):
                for i, (o, w) in enumerate(KCH):
                    w = min(w, NK - o)
                    pr.wait(pe_v, 4, 4 * n + i + 1)
                    copy(rawV[:, o:o + w], ST[i][:, 0:w]).then_inc(act_vraw, 1)

            def tiles_v(pr, n):
                for i in range(4):
                    pr.wait(pe_vt, 4, 4 * n + i + 1)
                    c = min(4, KT - 4 * i)
                    k = rows_of(4 * i + c - 1)
                    copy(V[0:k, 4 * i:4 * i + c, :], ST[i][0:k, 0:c * 128].rearrange("k (t d) -> k t d", d=128))\
                        .then_inc(act_v, 1)

            def take_o(pr, g, c2):
                pr.wait(pe_pv, 2 * STEPS, g * STEPS + (c2 + 1) * KT)
                pr.wait(dve_on, 8, 4 * g)
                copy(Oraw[:, c2, :], OB[:, :]).then_inc(act_o, 1)

            def attend(pr, g):
                for s in range(STEPS):
                    k = rows_of(s % KT)
                    for jj in range(2):
                        u = 2 * s + jj
                        pr.wait(pe_st, 2 * UNITS, g * UNITS + u + 1)
                        v = max(u - NP, -1) + 1
                        pr.wait(pe_pv, 2 * STEPS, g * STEPS + (v + 1) // 2)
                        pr.wait(pool_acc, 2 * UNITS, g * UNITS + v)
                        act.activation(P[0:k, u % NP, :], ST[u % 4][0:k, :], ACT.Exp, scale=SCALE).then_inc(act_p, 1)
                    if s == KT:
                        take_o(pr, g, 0)
                take_o(pr, g, 1)

            def pair(l, p, last):
                pr = Pair(act, act.snap(l * PAIRS + p), start)
                attend(pr, 0)
                if not last:
                    pr.wait(dve_lo, 4, 4)
                    raw_kq(pr, 1, range(0, 4))
                    pr.wait(pe_st, 2 * UNITS, UNITS)
                    hi_k(pr, 1, 2)
                    raw_kq(pr, 1, range(4, 8))
                    hi_q(pr, 1, 2)
                attend(pr, 1)
                if not last:
                    pr.wait(pe_st, 2 * UNITS, 2 * UNITS)
                    hi_k(pr, 1, 3)
                    raw_v(pr, 1)
                    hi_q(pr, 1, 3)
                    tiles_v(pr, 1)

            with act.Fori(0, LAYERS) as l:
                act.wait_ge(act_set, QT // 2 + KT + 1)
                act.wait_ge(dve_x, l * (8 * PAIRS) + 1)
                for j in range(JQ):
                    if j >= 2:
                        act.wait_ge(pe_sq, l * JQ + (j - 1))
                    for ct in range(CT):
                        last = act.activation(P[:, 2 * (j % 2) + ct, :], xacc[:, ct, j * 512:(j + 1) * 512], ACT.Square)
                    last.then_inc(act_sq, 1)
                act.wait_ge(dve_var, l * (JQ + 1) + (JQ + 1)) if False else None
                act.wait_ge(dve_own, l + 1)
                act.activation(On[:, :], On[:, :], ACT.Sqrt).then_inc(act_rms, 1)
                pr = Pair(act, act.snap(l * PAIRS), start)
                raw_kq(pr, 0, range(0, 4))
                act.wait_ge(d_ext, l * 64 + 64)
                hi_k(pr, 0, 0)
                raw_kq(pr, 0, range(4, 8))
                hi_q(pr, 0, 0)
                raw_v(pr, 0)
                tiles_v(pr, 0)
                hi_k(pr, 0, 1)
                hi_q(pr, 0, 1)
                with act.Fori(0, PAIRS - 1) as p:
                    pair(l, p, False)
                pair(l, PAIRS - 1, True)

        @block.vector
        def _(dve):
            for s in (dve_s, dve_mrow, dve_r, dve_x, dve_on, dve_m):
                dve.sem_inc(s, 1)
            for b in range(2):
                o = 64 * (1 - b)
                for m in (Q2[b], K2[b], KS[b]):
                    dve.memset(words(m[o:o + 64, :]), 0.0).then_inc(dve_zero, 1)
            dve.wait_ge(d_m, 16)
            m = xq[0:2, 0, :]
            dve.tensor_scalar(m, m, -1.0, 1.0, ALU.mult, ALU.add).then_inc(dve_set, 1)
            dve.wait_ge(dve_set, 1)
            dve.tensor_scalar(m, m, -SUPPRESS / SCALE, None, ALU.mult).then_inc(dve_bias, 1)
            dve.wait_ge(dve_bias, 1)
            dve.tensor_copy(Q1[0][0:2, :], m).then_inc(dve_bias, 1)
            dve.wait_ge(dve_bias, 2)
            dve.tensor_tensor(Q1[1][0:2, :], m, Q1[0][0:2, :], ALU.subtract).then_inc(dve_bias, 1)
            dve.wait_ge(pool_set, 4)
            dve.tensor_scalar(first_row[:, :], tok[:, 7:8].bitcast(I32), 0.0, None, ALU.is_equal).then_inc(dve_set, 1)
            dve.wait_ge(d_biasrow, 128)

            def lo_parts(pr, g):
                b = g % 2
                own, other = slice(64 * b, 64 * b + 64), slice(64 * (1 - b), 64 * (1 - b) + 64)
                pr.wait(act_hi, 10, 5 * (g + 1))
                dve.tensor_tensor(K2[b][own, :], rawK[own, :], K1[b][own, :], ALU.subtract).then_inc(dve_lo, 1)
                dve.tensor_tensor(Q1[b][other, :], rawQ[own, :], Q1[b][own, :], ALU.subtract).then_inc(dve_lo, 1)

            def s_max(pr, g, i):
                w = KCH[i % len(KCH)][1]
                if i == 0:
                    pr.wait(dve_m, 2, g)
                pr.wait(pe_s, 2 * SUNITS, g * SUNITS + i + 1)
                dve.tensor_reduce(mpart[:, i // len(KCH), i % len(KCH):i % len(KCH) + 1], SS[i % 2][:, 0:w],
                                  AX.X, ALU.max).then_inc(dve_s, 1)

            def head_max(pr, g):
                pr.wait(dve_s, 2 * SUNITS, (g + 1) * SUNITS)
                dve.tensor_reduce(negm[:, :], mpart[:, :, :], AX.X, ALU.max, negate=True).then_inc(dve_m, 1)

            def max_row(pr, g):
                pr.wait(pe_m, 2, g + 1)
                pr.wait(d_m, 32, 16 * g)
                dve.tensor_copy(mrow[:, :], SS[0][0:QT, 0:128]).then_inc(dve_mrow, 1)

            def reciprocals(pr, g, c2, piece):
                q = slice(piece * 128, piece * 128 + 128)
                if piece == 0:
                    pr.wait(dve_on, 8, 4 * g + 2 * c2)
                    pr.wait(pe_z, 4, 2 * g + c2 + 1)
                ins = dve.reciprocal(R[:, q], ZB[:, q])
                if piece == 3:
                    ins.then_inc(dve_r, 1)

            def divide(pr, g, c2):
                b = g % 2
                pr.wait(dve_r, 4, 2 * g + c2 + 1)
                pr.wait(act_o, 4, 2 * g + c2 + 1)
                if g == 0 and c2 == 0:
                    pr.wait(pe_o, 8, 0)
                for jj in range(2):
                    j, r = 2 * c2 + jj, slice(64 * jj, 64 * jj + 64)
                    dve.tensor_tensor(On[64 * b:64 * b + 64, j * 512:(j + 1) * 512], Oraw[r, c2, :], R[r, :],
                                      ALU.mult).then_inc(dve_on, 1)

            def normalise(pr, g, c2):
                for piece in range(4):
                    reciprocals(pr, g, c2, piece)
                divide(pr, g, c2)

            def attend(pr, g, other):
                for s in range(STEPS):
                    if other is not None:
                        for i in s_units(s):
                            s_max(pr, other, i)
                    if KT + 4 <= s < KT + 8:
                        reciprocals(pr, g, 0, s - KT - 4)
                    if s == KT + 8:
                        divide(pr, g, 0)

            def add_output(pr):
                for i in range(CT * JQ):
                    ct, j = i // JQ, i % JQ
                    pr.wait(pe_o, 8, i + 1)
                    x = xacc[:, ct, j * 512:(j + 1) * 512]
                    dve.tensor_tensor(x, ST[i % 4][:, :], x, ALU.add).then_inc(dve_x, 1)

            def pair(l, p, last):
                pr = Pair(dve, dve.snap(l * PAIRS + p), start)
                attend(pr, 0, 1)
                head_max(pr, 1)
                max_row(pr, 1)
                normalise(pr, 0, 1)
                if not last:
                    lo_parts(pr, 2)
                attend(pr, 1, None if last else 2)
                if not last:
                    head_max(pr, 2)
                    max_row(pr, 2)
                normalise(pr, 1, 1)
                if not last:
                    lo_parts(pr, 3)
                add_output(pr)

            dve.wait_ge(act_set, QT // 2 + KT + 1)
            with dve.Fori(0, LAYERS) as l:
                dve.wait_ge(d_layer, l * 80 + 80)
                TOK = 10
                def link(ins, k):
                    ins.then_inc(dve_tok, 1)
                    dve.wait_ge(dve_tok, l * TOK + k)
                key, hit, hit2 = rawK[0:NROWS, :], rawQ[0:NROWS, 0:KP], On[0:NROWS, 0:KP]
                link(dve.tensor_copy(tok[:, 0:4], tok_i[:, :]), 1)
                link(dve.tensor_scalar(R[0:NROWS, 0:4], tok[:, 0:4], 0.0, float(NK), ALU.is_lt, ALU.mult), 2)
                link(dve.tensor_tensor(tok[:, 0:4], tok[:, 0:4], R[0:NROWS, 0:4], ALU.add), 3)
                link(dve.tensor_scalar(hit, key, tok[:, 2:3], None, ALU.is_equal), 4)
                link(dve.scalar_tensor_tensor(hit, key, tok[:, 3:4], hit, ALU.is_equal, ALU.max), 5)
                link(dve.tensor_scalar(hit, hit, -1.0, 1.0, ALU.mult, ALU.add), 6)
                link(dve.tensor_scalar(hit2, key, tok[:, 0:1], None, ALU.is_equal), 7)
                link(dve.scalar_tensor_tensor(hit2, key, tok[:, 1:2], hit2, ALU.is_equal, ALU.max), 8)
                link(dve.tensor_tensor(hit2, hit2, hit, ALU.mult), 9)
                dve.wait_ge(pe_st, l * (HEADS * UNITS) + 1)
                dve.tensor_scalar(K1[1][0:NROWS, :], hit2, first_row[:, 0:1], None, ALU.add).then_inc(dve_tok, 1)
                dve.wait_ge(dve_tok, l * TOK + TOK)
                for j in range(JQ):
                    dve.wait_ge(pe_sq, l * JQ + (j + 1))
                    dve.tensor_scalar(rawQ[:, j * 512:(j + 1) * 512], ST[j][:, :], 1.0 / C, EPS, ALU.mult, ALU.add)\
                        .then_inc(dve_var, 1)
                dve.wait_ge(dve_var, l * JQ + JQ)
                dve.reciprocal(On[:, :], rawQ[:, :]).then_inc(dve_own, 1)
                dve.wait_ge(act_rms, l + 1)
                dve.tensor_scalar(rawQ[:, :], On[:, :], ab[:, 0:1], ab[:, 1:2], ALU.mult, ALU.add).then_inc(dve_ext, 1)
                dve.wait_ge(dve_ext, l + 1)
                for ct in range(CT):
                    last = dve.scalar_tensor_tensor(xq[:, ct, :], xacc[:, ct, :], nw[:, ct:ct + 1], rawQ[:, :],
                                                    ALU.mult, ALU.mult)
                last.then_inc(dve_xq, 1)
                dve.wait_ge(dve_xq, l + 1)
                for ct in range(CT):
                    last = dve.tensor_scalar(xacc[:, ct, :], xacc[:, ct, :], bo[:, ct:ct + 1], None, ALU.add)
                last.then_inc(dve_bo, 1)
                dve.wait_ge(dve_bo, l + 1)
                pr = Pair(dve, dve.snap(l * PAIRS), start)
                lo_parts(pr, 0)
                for i in range(SUNITS):
                    s_max(pr, 0, i)
                head_max(pr, 0)
                max_row(pr, 0)
                lo_parts(pr, 1)
                with dve.Fori(0, PAIRS - 1) as p:
                    pair(l, p, False)
                pair(l, PAIRS - 1, True)

            for t in range(QT):
                dve.wait_ge(pe_out, t + 1)
                dve.tensor_copy(x_out[:, t, :], ST[t % 4][:, 0:C]).then_inc(dve_out, 1)


def kernel(**inp):
    import concourse.bacc as bacc
    from concourse.bass_utils import run_bass_kernel_spmd as run

    big = {0: "L0_xattn_", 2: "L2_xattn_", 3: "L3_xattn_"}
    f = np.float32
    wq = np.zeros((LAYERS, C, HEADS, D), f)
    wk = np.zeros((LAYERS, CC, HEADS, D), f)
    wv = np.zeros((LAYERS, CC, HEADS, D), f)
    wo = np.zeros((LAYERS, HEADS, D, C), f)
    bo = np.zeros((LAYERS, C), f)
    nw = np.ones((LAYERS, C), f)
    tok = np.full((LAYERS, NROWS, 4), NONE, np.int32)
    ab = np.zeros((LAYERS, P128, 2), f)
    for l, k in big.items():
        wq[l] = np.asarray(inp[k + "Wq"]).reshape(C, HEADS, D)
        wk[l] = np.asarray(inp[k + "Wk"]).reshape(CC, HEADS, D)
        wv[l] = np.asarray(inp[k + "Wv"]).reshape(CC, HEADS, D)
        wo[l] = np.asarray(inp[k + "Wo"]).reshape(HEADS, D, C)
        bo[l] = np.asarray(inp[k + "bo"])
        A, B = np.asarray(inp[k + "token_indices_A"]), np.asarray(inp[k + "token_indices_B"])
        tok[l, 1:3, 0:2] = A
        tok[l, 1:3, 2:4] = B
        tok[l, 3:5, 0:2] = B
        ab[l, :, 1] = 1.0
    d1 = C // HEADS
    groups = np.asarray(inp["L1_xattn_wk"]).shape[1] // d1
    rep = HEADS // groups
    wq[1, :, :, :d1] = np.asarray(inp["L1_xattn_wq"]).reshape(C, HEADS, d1)
    for h in range(HEADS):
        g = h // rep
        wk[1, :, h, :d1] = np.asarray(inp["L1_xattn_wk"])[:, g * d1:(g + 1) * d1]
        wv[1, :, h, :d1] = np.asarray(inp["L1_xattn_wv"])[:, g * d1:(g + 1) * d1]
    wo[1, :, :d1] = np.asarray(inp["L1_xattn_wo"]).reshape(HEADS, d1, C)
    nw[1] = np.asarray(inp["L1_xattn_norm_w"])
    ab[1, :, 0] = 2.0

    def columns(w, n):
        w = w.reshape(LAYERS, n, P128, PAIRS, 2 * D).transpose(0, 3, 2, 1, 4).reshape(LAYERS * PAIRS, P128, n, 2 * D)
        return np.ascontiguousarray(np.concatenate([w, w[:1]]))

    def vectors(v):
        return np.ascontiguousarray(v.reshape(LAYERS, CT, P128).transpose(0, 2, 1))

    wo = wo.reshape(LAYERS * PAIRS, 2 * D, C)
    arrays = {
        "x": np.ascontiguousarray(np.asarray(inp["x"])[0]),
        "ctx": np.ascontiguousarray(np.asarray(inp["ctx_2048"])[0]),
        "mask": np.stack([np.asarray(inp["mask_S_fk1"]), np.asarray(inp["mask_S_fk0"])]),
        "wq": columns(wq, CT), "wk": columns(wk, CCT), "wv": columns(wv, CCT),
        "wo": np.ascontiguousarray(np.concatenate([wo, wo[:1]])),
        "bo": vectors(bo), "nw": vectors(nw), "tok": tok, "ab": ab,
        "key": np.tile(np.minimum(np.arange(KP), NK - 1).astype(f), (NROWS, 1)),
    }
    nc = bacc.Bacc("TRN2", target_bir_lowering=False, num_devices=1)
    aps = {k: nc.dram_tensor(f"in_{k}", v.shape, mybir.dt.from_np(v.dtype), kind="ExternalInput").ap()
           for k, v in arrays.items()}
    aps["out"] = nc.dram_tensor("out", (NQ, C), F32, kind="ExternalOutput").ap()
    attention_layers(nc, aps)
    r = run(nc, [{f"in_{k}": v for k, v in arrays.items()}], core_ids=[0])
    return r.results[0]["out"].reshape(1, NQ, C)
```

```python
from contextlib import ExitStack

import numpy as np
import concourse.bass as bass
from concourse import mybir
from concourse.alu_op_type import AluOpType as ALU

F32 = mybir.dt.float32
F32R = mybir.dt.float32r
I32 = mybir.dt.int32
ACT = mybir.ActivationFunctionType
AX = mybir.AxisListType

P128 = 128
BIG, HEADS, D = 3, 16, 64
GROUPS, D1 = 4, 16
ROUNDS = HEADS // GROUPS
NQ, NK, C, CC = 2048, 1601, 256, 512
PAIRS = HEADS // 2
QT, KT = NQ // P128, -(-NK // P128)
KREST = NK - (KT - 1) * P128
KP = NK + 1
KCH = [(0, 402), (402, 400), (802, 400), (1202, 400)]
TOK = 10
JQ = NQ // 512
CT, CCT = C // P128, CC // P128
NP = 6
STEPS = 2 * KT
UNITS = 2 * STEPS
SUNITS = QT * len(KCH)
SUPPRESS, SCALE, EPS = 20.0, 0.125, 1e-5
NROWS = 5
NONE = 4096
SCALE1 = D1 ** -0.5
QD = 32
MROW = 3 * QD + D1
GUNITS = KT * JQ
GSTEPS = range(1, KT - 2)


def s_units(step):
    first, steps = 2, STEPS - 2
    if step < first:
        return range(0)
    a, b = step - first, step - first + 1
    return range(a * SUNITS // steps, b * SUNITS // steps)


def g_s_units(t):
    if t not in GSTEPS:
        return []
    a = t - GSTEPS.start
    return list(range(a * SUNITS // len(GSTEPS), (a + 1) * SUNITS // len(GSTEPS)))


def number(eng, v):
    return v if isinstance(v, int) else eng.snap(v)


def words(ap):
    return ap.bitcast(F32)


def rows_of(t):
    return KREST if t == KT - 1 else P128


class Pair:

    def __init__(self, eng, n, start, ahead=()):
        self.eng, self.n, self.start, self.made = eng, n, start, {}
        self.ahead = {(m, c): number(eng, n * m + c) for m, c in ahead}

    def wait(self, sem, per_pair, plus):
        plus += self.start.get(sem.name, 0)
        if (per_pair, plus) in self.ahead:
            self.eng.wait_ge(sem, self.ahead[per_pair, plus])
            return
        if per_pair not in self.made:
            self.made[per_pair] = number(self.eng, self.n * per_pair)
        self.eng.wait_ge(sem, self.made[per_pair] + plus)


def attention_layers(nc, a):
    with ExitStack() as ctx:
        def sb(name, shape, dt=F32):
            return ctx.enter_context(nc.sbuf_tensor(name, shape, dt))

        start = {}

        def sem(name):
            return ctx.enter_context(nc.semaphore(name))

        def from_one(name):
            start[name] = 1
            return sem(name)

        ctxT = sb("ctxT", [128, CCT, KP])
        xacc = sb("xacc", [128, CT, NQ])
        xq = sb("xq", [128, CT, NQ])
        ident = sb("ident", [128, 128])
        ones = sb("ones", [128, 128])
        wk = sb("wk", [128, CCT, 128])
        wv = sb("wv", [128, CCT, 128])
        wq = sb("wq", [128, CT, 128])
        wo = sb("wo", [128, C])
        rawK = sb("rawK", [128, KP])
        rawQ = sb("rawQ", [128, NQ])
        rawV = sb("rawV", [128, NK])
        V = sb("V", [128, KT, 128])
        Q1 = [sb(f"Q1_{b}", [128, NQ], F32R) for b in range(2)]
        Q2 = [sb(f"Q2_{b}", [128, NQ], F32R) for b in range(2)]
        K1 = [sb(f"K1_{b}", [128, KP], F32R) for b in range(2)]
        K2 = [sb(f"K2_{b}", [128, KP], F32R) for b in range(2)]
        KS = [sb(f"KS_{b}", [128, KP], F32R) for b in range(2)]
        P = sb("P", [128, NP, 512])
        acc = sb("acc", [128, 2, 2, 512])
        Oraw = sb("Oraw", [128, 2, 512])
        R = sb("R", [128, 512])
        On = sb("On", [128, NQ])
        mpart = sb("mpart", [128, QT, len(KCH)])
        negm = sb("negm", [128, QT])
        mrow = sb("mrow", [QT, 128], F32R)
        tok_i = sb("tok_i", [NROWS, 4], I32)
        tok = sb("tok", [NROWS, 8])
        first_row = sb("first_row", [NROWS, 1])
        nw = sb("nw", [128, CT])
        bo = sb("bo", [128, CT])
        sel = sb("sel", [128, 128])
        KG = [K1[0], K1[1], K2[0], K2[1]]
        gwk, gwv = (rawK[:, i * CCT * 128:(i + 1) * CCT * 128].rearrange("p (t m) -> p t m", m=128) for i in range(2))
        gwq = rawK[:, 2 * CCT * 128:(2 * CCT + CT) * 128].rearrange("p (t m) -> p t m", m=128)
        gwo = rawK[:, (2 * CCT + CT) * 128:(2 * CCT + CT) * 128 + C]
        K4hi = P[:, :, :].rearrange("p n q -> p (n q)")[:, 0:KP].bitcast(F32R)
        K4lo = acc[:, :, :, :].rearrange("p a b q -> p (a b q)")[:, 0:KP].bitcast(F32R)
        Q4hi, Q4lo = Q2[0], rawQ[:, :].bitcast(F32R)
        PG = [P[:, i, :] for i in range(NP)] + [acc[:, i // 2, i % 2, :] for i in range(4)]

        ST = [ctx.enter_context(nc.psum_tensor(f"ST{i}", [128, 512], F32)) for i in range(4)]
        SS = [ctx.enter_context(nc.psum_tensor(f"SS{i}", [128, 512], F32)) for i in range(2)]
        OB = ctx.enter_context(nc.psum_tensor("OB", [128, 512], F32))
        ZB = ctx.enter_context(nc.psum_tensor("ZB", [128, 512], F32))
        GB = [SS[0], SS[1], OB, ZB]

        d_in = sem("d_in")
        d_biasrow = sem("d_biasrow")
        d_layer = sem("d_layer")
        d_ext = sem("d_ext")
        d_out = sem("d_out")
        pool_set = sem("pool_set")
        pe_set = sem("pe_set")
        act_set = sem("act_set")
        dve_set = sem("dve_set")
        dve_zero = sem("dve_zero")
        dve_bias = sem("dve_bias")
        dve_tok = sem("dve_tok")
        dve_xq = sem("dve_xq")
        dve_bo = sem("dve_bo")
        pe_out = sem("pe_out")
        dve_out = sem("dve_out")
        d_wkq, d_wv, d_wo = sem("d_wkq"), sem("d_wv"), sem("d_wo")
        pe_kq = sem("pe_kq")
        act_kq = sem("act_kq")
        pe_v = sem("pe_v")
        act_vraw = sem("act_vraw")
        pe_vt = sem("pe_vt")
        act_v = sem("act_v")
        pe_o = from_one("pe_o")
        dve_x = from_one("dve_x")
        act_hi = sem("act_hi")
        dve_lo = sem("dve_lo")
        pe_s = sem("pe_s")
        dve_s = from_one("dve_s")
        dve_m = from_one("dve_m")
        pe_m = sem("pe_m")
        dve_mrow = from_one("dve_mrow")
        d_m = sem("d_m")
        pe_st = from_one("pe_st")
        act_p = sem("act_p")
        pool_acc = from_one("pool_acc")
        pe_pv = from_one("pe_pv")
        act_o = from_one("act_o")
        pe_z = from_one("pe_z")
        dve_r = from_one("dve_r")
        dve_on = from_one("dve_on")

        start["d_m"] = 16

        gd_load = sem("gd_load")
        gd_k = sem("gd_k")
        act_sq, pe_sq, dve_var = sem("act_sq"), sem("pe_sq"), sem("dve_var")
        dve_inv, act_rms, g_xq = sem("dve_inv"), sem("act_rms"), sem("g_xq")
        pool_ones = sem("pool_ones")
        dve_sel = sem("dve_sel")
        gpe_k, gact_k, gdve_k = sem("gpe_k"), sem("gact_k"), sem("gdve_k")
        gpe_v, gact_vraw, gpe_vt, gact_v = sem("gpe_v"), sem("gact_vraw"), sem("gpe_vt"), sem("gact_v")
        pool_clear = sem("pool_clear")
        gd_bias = sem("gd_bias")
        gd_wq, gd_wo = sem("gd_wq"), sem("gd_wo")
        gpe_q, gact_q, gdve_q = sem("gpe_q"), sem("gact_q"), sem("gdve_q")
        gpe_o, gdve_x = sem("gpe_o"), sem("gdve_x")
        gd_q = sem("gd_q")
        gpe_s, gdve_s = sem("gpe_s"), sem("gdve_s")
        gdve_m, gpe_m, gdve_mrow = sem("gdve_m"), sem("gpe_m"), sem("gdve_mrow")
        gd_m = sem("gd_m")
        gpe_st, gact_p = sem("gpe_st"), sem("gact_p")
        gpe_pv = sem("gpe_pv")
        gact_o, gpe_z, gdve_r = sem("gact_o"), sem("gpe_z"), sem("gdve_r")
        gpool_on = sem("gpool_on")

        block = ctx.enter_context(nc.Block())

        x_land = [rawQ[:, :].rearrange("p (t c) -> p t c", c=C), On[:, :].rearrange("p (t c) -> p t c", c=C)]
        ctx_land = [P[:, i, :] for i in range(6)] + [acc[:, i // 2, i % 2, :] for i in range(4)] \
            + [Oraw[:, i, :] for i in range(2)] + [R[0:KREST, :]]
        XH = QT // 2
        x_out = xq[:, :, :].rearrange("p a b -> p (a b)").rearrange("p (t c) -> p t c", c=C)

        @block.sync
        def _(sp):
            for i in range(2):
                sp.dma_start(x_land[i], a["x"][i * XH * 128:(i + 1) * XH * 128, :]
                             .rearrange("(t p) c -> p t c", p=128)).then_inc(d_in, 16)
            sp.dma_start(P[:, :, :], a["ctx"][0:768, :].rearrange("(t p) c -> p t c", p=128)).then_inc(d_in, 16)
            sp.dma_start(acc[:, :, :, :].rearrange("p a b c -> p (a b) c"),
                         a["ctx"][768:1280, :].rearrange("(t p) c -> p t c", p=128)).then_inc(d_in, 16)
            sp.dma_start(Oraw[:, :, :], a["ctx"][1280:1536, :].rearrange("(t p) c -> p t c", p=128)).then_inc(d_in, 16)
            sp.dma_start(R[0:KREST, :], a["ctx"][1536:NK, :]).then_inc(d_in, 16)
            sp.dma_start(xq[0:2, 0, :], a["mask"][:, :]).then_inc(d_m, 16)
            sp.dma_start(wk[:, :, :], a["wk"][0, :, :, :]).then_inc(d_wkq, 16)
            sp.dma_start(wq[:, :, :], a["wq"][0, :, :, :]).then_inc(d_wkq, 16)
            sp.dma_start(wv[:, :, :], a["wv"][0, :, :, :]).then_inc(d_wv, 16)
            sp.dma_start(wo[:, :], a["wo"][0, :, :]).then_inc(d_wo, 16)
            sp.wait_ge(dve_bias, 3)
            sp.wait_ge(dve_zero, 6)
            for b in range(2):
                o = 64 * (1 - b)
                for r in range(4):
                    sp.dma_start(words(Q2[b][o + 1 + r:o + 2 + r, :]), words(Q1[r % 2][r // 2:r // 2 + 1, :])).then_inc(d_biasrow, 16)
            sp.wait_ge(d_biasrow, 128)

            def load_kq(n):
                sp.dma_start(wk[:, :, :], a["wk"][n, :, :, :]).then_inc(d_wkq, 16)
                sp.dma_start(wq[:, :, :], a["wq"][n, :, :, :]).then_inc(d_wkq, 16)

            def max_row(b, pr, g):
                pr.wait(dve_mrow, 2, g + 1)
                o = 64 * (1 - b)
                sp.dma_start(words(Q2[b][o:o + 1, :]).rearrange("o (t p) -> o t p", p=128), words(mrow[:, :])).then_inc(d_m, 16)

            def pair(l, p, last):
                n = number(sp, l * PAIRS + p)
                n1, n2 = number(sp, n + 1), number(sp, n + 2)
                pr = Pair(sp, n, start, [(2, 3), (8, 9)] + ([] if last else [(8, 16), (2, 4), (4, 8)]))
                max_row(1, pr, 1)
                if not last:
                    pr.wait(pe_kq, 8, 16)
                    load_kq(n2)
                    max_row(0, pr, 2)
                    pr.wait(pe_v, 4, 8)
                    sp.dma_start(wv[:, :, :], a["wv"][n2, :, :, :]).then_inc(d_wv, 16)
                pr.wait(pe_o, 8, 8)
                sp.dma_start(wo[:, :], a["wo"][n1, :, :]).then_inc(d_wo, 16)

            def big_layer(l):
                n0 = number(sp, l * PAIRS)
                n1 = number(sp, n0 + 1)
                written, rows_made = number(sp, l * (8 * PAIRS) + 1), number(sp, l * TOK + TOK)
                pr = Pair(sp, n0, start, [(8, 8), (4, 4), (2, 2)])
                sp.wait_ge(pe_o, written)
                sp.dma_start(rawK[0:NROWS, :], a["key"][:, :]).then_inc(d_layer, 16)
                sp.dma_start(tok_i[:, :], a["tok"][l, :, :]).then_inc(d_layer, 16)
                sp.dma_start(bo[:, :], a["bo"][l, :, :]).then_inc(d_layer, 16)
                sp.wait_ge(dve_tok, rows_made)
                for b in range(2):
                    o = 64 * (1 - b)
                    sp.dma_start(words(K2[b][o:o + NROWS, :]), words(K1[1][0:NROWS, :])).then_inc(d_ext, 16)
                    sp.dma_start(words(KS[b][o + 1:o + NROWS, :]), words(K1[1][1:NROWS, :])).then_inc(d_ext, 16)
                pr.wait(pe_kq, 8, 8)
                load_kq(n1)
                pr.wait(pe_v, 4, 4)
                sp.dma_start(wv[:, :, :], a["wv"][n1, :, :, :]).then_inc(d_wv, 16)
                max_row(0, pr, 0)
                with sp.Fori(0, PAIRS - 1) as p:
                    pair(l, p, False)
                pair(l, PAIRS - 1, True)

            def stack(to, hi, lo, order, done):
                for i, part in enumerate(order):
                    rows = QD if i < 3 else D1
                    src = (hi, lo)[part]
                    sp.dma_start(words(to[i * QD:i * QD + rows, :]), src[0:rows, :]).then_inc(done, 16)

            def group_q(pr, h):
                g = h % GROUPS
                if g == 0:
                    pr.wait(gdve_q, 4, 4 * (h // GROUPS + 1))
                elif h >= 2:
                    pr.wait(gpe_st, GROUPS * GUNITS, (h - 1) * GUNITS)
                q = slice(g * QD, g * QD + QD)
                stack(Q1[h % 2], words(Q4hi[q, :]), words(Q4lo[q, :]), (0, 1, 0, 1), gd_q)

            def group_max(pr, h):
                pr.wait(gdve_mrow, GROUPS, h + 1)
                sp.dma_start(words(Q1[h % 2][MROW:MROW + 1, :]).rearrange("o (t p) -> o t p", p=128),
                             words(mrow[:, :])).then_inc(gd_m, 16)

            def group_layer():
                sp.wait_ge(dve_x, 8 * PAIRS + 1)
                sp.dma_start(gwk, a["gwk"][:, :, :]).then_inc(gd_load, 16)
                sp.dma_start(gwv, a["gwv"][:, :, :]).then_inc(gd_load, 16)
                sp.dma_start(nw[:, :], a["nw"][:, :]).then_inc(gd_load, 16)
                sp.dma_start(gwq, a["gwq"][0, :, :, :]).then_inc(gd_wq, 16)
                sp.dma_start(gwo, a["gwo"][0, :, :]).then_inc(gd_wo, 16)
                sp.wait_ge(pool_ones, GROUPS + 1)
                sp.wait_ge(gdve_k, 4)
                for g in range(GROUPS):
                    k = slice(g * QD, g * QD + QD)
                    stack(KG[g], words(K4hi[k, :]), words(K4lo[k, :]), (0, 0, 1, 1), gd_k)
                pr = Pair(sp, 0, start)
                group_q(pr, 0)
                sp.dma_start(gwq, a["gwq"][1, :, :, :]).then_inc(gd_wq, 16)
                group_max(pr, 0)
                group_q(pr, 1)
                group_max(pr, 1)
                with sp.Fori(0, ROUNDS - 1) as r:
                    r1, r2 = sp.snap(r + 1), sp.snap(r + 2)
                    heads = range(2, 2 + GROUPS)
                    pr = Pair(sp, r, start, [(GROUPS * GUNITS, (h - 1) * GUNITS) for h in heads]
                              + [(GROUPS, h + 1) for h in heads] + [(4, 8), (8, 8)])
                    for h in heads:
                        group_q(pr, h)
                        if h == GROUPS:
                            sp.dma_start(gwq, a["gwq"][r2, :, :, :]).then_inc(gd_wq, 16)
                        group_max(pr, h)
                    pr.wait(gpe_o, 8, 8)
                    sp.dma_start(gwo, a["gwo"][r1, :, :]).then_inc(gd_wo, 16)
                pr = Pair(sp, ROUNDS - 1, start)
                for h in range(2, GROUPS):
                    group_q(pr, h)
                    group_max(pr, h)
                sp.wait_ge(pool_clear, 3)
                sp.dma_start(words(Q2[0][64 + 1:64 + NROWS, :]), words(Q2[1][1:NROWS, :])).then_inc(gd_bias, 16)
                sp.wait_ge(gd_bias, 16)

            big_layer(0)
            group_layer()
            with sp.Fori(0, BIG - 1) as l:
                big_layer(sp.snap(l + 1))

            for t in range(0, QT, 4):
                sp.wait_ge(dve_out, t + 4)
                sp.dma_start(a["out"][t * 128:(t + 4) * 128, :].rearrange("(t p) c -> p t c", p=128),
                             x_out[:, t:t + 4, :]).then_inc(d_out, 16)
            sp.wait_ge(d_out, 16 * QT // 4)
            sp.wait_ge(d_wkq, 32 * (BIG * PAIRS + 1))
            sp.wait_ge(d_wv, 16 * (BIG * PAIRS + 1))
            sp.wait_ge(d_wo, 16 * (BIG * PAIRS + 1))
            sp.wait_ge(gd_wq, 16 * (ROUNDS + 1))

        @block.gpsimd
        def _(gp):
            gp.sem_inc(pool_acc, 1)
            gp.memset(ident[:, :], 0.0).then_inc(pool_set, 1)
            gp.wait_ge(pool_set, 1)
            gp.affine_select(out=ident[:, :], in_=ident[:, :], compare_op=ALU.not_equal, fill=1.0, base=0,
                             pattern=[[-1, 128]], channel_multiplier=1).then_inc(pool_set, 1)
            gp.memset(ones[:, :], 1.0).then_inc(pool_set, 1)
            gp.wait_ge(pool_set, 3)
            gp.iota(tok[:, 7:8].bitcast(I32), [[0, 1]], base=0, channel_multiplier=1).then_inc(pool_set, 1)

            def head(pr, g):
                for u in range(UNITS):
                    c2, t, jj = u // (2 * KT), u // 2 % KT, u % 2
                    if t == 0:
                        continue
                    k = rows_of(t)
                    out = acc[0:k, c2, jj, :]
                    pr.wait(act_p, 2 * UNITS, g * UNITS + u + 1)
                    if t == 1:
                        pr.wait(pe_z, 4, 2 * g)
                        gp.tensor_tensor(out, P[:, (u - 2) % NP, :], P[:, u % NP, :], ALU.add)\
                            .then_inc(pool_acc, 1 + 2 * jj)
                    else:
                        pr.wait(pool_acc, 2 * UNITS, g * UNITS + u - 1)
                        gp.tensor_tensor(out, out, P[0:k, u % NP, :], ALU.add).then_inc(pool_acc, 1)

            def heads(pairs, first):
                with gp.Fori(0, pairs) as n:
                    pr = Pair(gp, n if first == 0 else gp.snap(n + first), start)
                    for g in range(2):
                        head(pr, g)

            def group_divide(pr, h):
                g = h % GROUPS
                pr.wait(gdve_r, GROUPS, h + 1)
                if g == 0 and h > 0:
                    pr.wait(gpe_o, 8, 8 * (h // GROUPS))
                for j in range(JQ):
                    q = slice(j * QD, j * QD + QD)
                    gp.tensor_tensor(On[g * QD:g * QD + QD, j * 512:(j + 1) * 512], Oraw[q, h % 2, :], R[q, :],
                                     ALU.mult).then_inc(gpool_on, 1)

            heads(PAIRS, 0)
            gp.wait_ge(dve_x, 8 * PAIRS + 1)
            for k in KG:
                gp.memset(words(k[3 * QD:4 * QD, :]), 1.0).then_inc(pool_ones, 1)
            gp.wait_ge(pool_ones, GROUPS)
            gp.memset(V[:, :, :].rearrange("p t (g d) -> p (t g) d", g=GROUPS)[:, :, D1:QD], 1.0).then_inc(pool_ones, 1)
            group_divide(Pair(gp, 0, start), 0)
            with gp.Fori(0, ROUNDS - 1) as r:
                pr = Pair(gp, r, start)
                for h in range(1, 1 + GROUPS):
                    group_divide(pr, h)
            pr = Pair(gp, ROUNDS - 1, start)
            for h in range(1, GROUPS):
                group_divide(pr, h)
            gp.wait_ge(gdve_x, 8 * ROUNDS)
            for m, o in ((Q2[0], 64), (K2[0], 64), (K2[1], 0)):
                gp.memset(words(m[o:o + 64, :]), 0.0).then_inc(pool_clear, 1)
            heads((BIG - 1) * PAIRS, PAIRS)

        @block.tensor
        def _(pe):
            for s in (pe_z, pe_pv, pe_o, pe_st):
                pe.sem_inc(s, 1)
            pe.wait_ge(pool_set, 3)
            pe.wait_ge(d_in, 96)
            for i in range(QT // 2):
                if i >= 4:
                    pe.wait_ge(act_set, i - 3)
                for k in range(4):
                    t, ct = 2 * i + k // 2, k % 2
                    last = pe.transpose(ST[i % 4][:, k * 128:(k + 1) * 128],
                                        x_land[t // XH][:, t % XH, ct * 128:(ct + 1) * 128], ident[:, :])
                last.then_inc(pe_set, 1)
            for t in range(KT):
                i = QT // 2 + t
                pe.wait_ge(act_set, i - 3)
                k = rows_of(t)
                for ct in range(CCT):
                    last = pe.transpose(ST[i % 4][:, ct * 128:ct * 128 + k],
                                        ctx_land[t][0:k, ct * 128:(ct + 1) * 128], ident[0:k, 0:k])
                last.then_inc(pe_set, 1)
            NSET = QT // 2 + KT + 1

            def project_kq(pr, n, first_waits):
                pr.wait(d_wkq, 32, 32 * (n + 1))
                for i in range(8):
                    if i < 4:
                        if i == 0:
                            first_waits()
                    else:
                        pr.wait(act_kq, 8, 8 * n + i - 3)
                    b = ST[i % 4]
                    if i < 4:
                        o, w = KCH[i]
                        for ct in range(CCT):
                            last = pe.matmul(b[:, 0:w], wk[:, ct, :], ctxT[:, ct, o:o + w],
                                             start=ct == 0, stop=ct == CCT - 1)
                    else:
                        j = i - 4
                        for ct in range(CT):
                            last = pe.matmul(b[:, :], wq[:, ct, :], xq[:, ct, j * 512:(j + 1) * 512],
                                             start=ct == 0, stop=ct == CT - 1)
                    last.then_inc(pe_kq, 1)
                    if i == 3:
                        yield

            def project_v(pr, n, first_waits):
                pr.wait(d_wv, 16, 16 * (n + 1))
                for i, (o, w) in enumerate(KCH):
                    first_waits(i)
                    w = min(w, NK - o)
                    for ct in range(CCT):
                        last = pe.matmul(ST[i][:, 0:w], wv[:, ct, :], ctxT[:, ct, o:o + w],
                                         start=ct == 0, stop=ct == CCT - 1)
                    last.then_inc(pe_v, 1)

            def transpose_v(pr, n):
                pr.wait(act_vraw, 4, 4 * (n + 1))
                for i in range(4):
                    for t in range(4 * i, min(4 * i + 4, KT)):
                        k, c = rows_of(t), t - 4 * i
                        last = pe.transpose(ST[i][0:k, c * 128:(c + 1) * 128], rawV[:, t * 128:t * 128 + k], ident[:, :])
                    last.then_inc(pe_vt, 1)

            def s_tile(pr, g, i):
                b = g % 2
                if i == 0:
                    pr.wait(act_hi, 10, 5 * (g + 1))
                    pr.wait(dve_mrow, 2, g)
                    pr.wait(dve_s, 2 * SUNITS, g * SUNITS)
                if i >= 2:
                    pr.wait(dve_s, 2 * SUNITS, g * SUNITS + i - 1)
                qt, (o, w) = i // len(KCH), KCH[i % len(KCH)]
                pe.matmul(SS[i % 2][:, 0:w], Q2[b][:, qt * 128:(qt + 1) * 128], KS[b][:, o:o + w],
                          start=True, stop=True).then_inc(pe_s, 1)

            def transpose_max(pr, g):
                pr.wait(dve_m, 2, g + 1)
                pe.transpose(SS[0][0:QT, 0:128], negm[:, :], ident[:, :]).then_inc(pe_m, 1)

            def sums(pr, g, c2):
                pr.wait(pool_acc, 2 * UNITS, g * UNITS + (c2 + 1) * 2 * KT)
                pr.wait(dve_r, 4, 2 * g + c2)
                for jj in range(2):
                    last = pe.matmul(ZB[64 * jj:64 * jj + 64, :], ones[:, 0:64], acc[:, c2, jj, :],
                                     start=True, stop=True)
                last.then_inc(pe_z, 1)

            def attend(pr, g, first_waits, other):
                b = g % 2

                def scores(s, jj):
                    c2, t = s // KT, s % KT
                    k, u, j = rows_of(t), 2 * s + jj, 2 * c2 + jj
                    if u >= 4:
                        pr.wait(act_p, 2 * UNITS, g * UNITS + u - 3)
                    bank = ST[u % 4][0:k, :]
                    pe.matmul(bank, K1[b][:, t * 128:t * 128 + k], Q1[b][:, j * 512:(j + 1) * 512],
                              start=True, stop=False)
                    pe.matmul(bank, K2[b][:, t * 128:t * 128 + k], Q2[b][:, j * 512:(j + 1) * 512],
                              start=False, stop=True).then_inc(pe_st, 1)

                def s_next(tiles, last=False):
                    for i in tiles if last else tiles[:1]:
                        s_tile(pr, other, i)
                    return tiles[1:]

                first_waits()
                pr.wait(act_hi, 10, 5 * (g + 1))
                pr.wait(dve_lo, 4, 2 * (g + 1))
                pr.wait(d_m, 32, 16 * (g + 1))
                for jj in range(2):
                    scores(0, jj)
                for s in range(STEPS):
                    c2, t = s // KT, s % KT
                    k = rows_of(t)
                    tiles = [] if other is None else list(s_units(s))
                    for jj in range(2):
                        if s + 1 < STEPS:
                            scores(s + 1, jj)
                        tiles = s_next(tiles)
                    pr.wait(act_p, 2 * UNITS, g * UNITS + 2 * s + 2)
                    if t == 0:
                        pr.wait(act_o, 4, 2 * g + c2)
                    for jj in range(2):
                        last = pe.matmul(OB[64 * jj:64 * jj + 64, :], V[0:k, t, 64 * b:64 * b + 64],
                                         P[0:k, (2 * s + jj) % NP, :], start=t == 0, stop=t == KT - 1)
                    last.then_inc(pe_pv, 1)
                    s_next(tiles, last=True)
                    if s == KT + 3:
                        sums(pr, g, 0)

            def output(pr, first_waits):
                pr.wait(d_wo, 16, 16)
                pr.wait(dve_on, 8, 8)
                for i in range(CT * JQ):
                    ct, j = i // JQ, i % JQ
                    if i == 0:
                        first_waits()
                    if i >= 4:
                        pr.wait(dve_x, 8, i - 3)
                    pe.matmul(ST[i % 4][:, :], wo[:, ct * 128:(ct + 1) * 128], On[:, j * 512:(j + 1) * 512],
                              start=True, stop=True).then_inc(pe_o, 1)

            def pair(l, p, last):
                pr = Pair(pe, number(pe, l * PAIRS + p), start)

                def before_a():
                    pr.wait(dve_x, 8, 0)
                    pr.wait(act_v, 4, 4)
                attend(pr, 0, before_a, 1)
                if last:
                    transpose_max(pr, 1)
                    sums(pr, 0, 1)
                else:
                    kq = project_kq(pr, 1, lambda: pr.wait(act_p, 2 * UNITS, UNITS))
                    next(kq)
                    transpose_max(pr, 1)
                    sums(pr, 0, 1)
                    for _ in kq:
                        pass
                attend(pr, 1, lambda: pr.wait(act_kq, 8, 8 if last else 16), None if last else 2)
                if last:
                    sums(pr, 1, 1)
                    output(pr, lambda: pr.wait(act_p, 2 * UNITS, 2 * UNITS))
                else:
                    project_v(pr, 1, lambda i: pr.wait(act_p, 2 * UNITS, 2 * UNITS) if i == 0 else None)
                    transpose_max(pr, 2)
                    sums(pr, 1, 1)
                    transpose_v(pr, 1)
                    output(pr, lambda: pr.wait(act_v, 4, 8))

            def big_layer(l):
                pe.wait_ge(act_set, NSET)
                pe.wait_ge(dve_x, number(pe, l * (8 * PAIRS) + 1))
                pr = Pair(pe, number(pe, l * PAIRS), start)
                kq = project_kq(pr, 0, lambda: None)
                next(kq)
                pe.wait_ge(dve_xq, number(pe, l + 1))
                for _ in kq:
                    pass
                project_v(pr, 0, lambda i: pr.wait(act_kq, 8, 5 + i))
                transpose_v(pr, 0)
                pe.wait_ge(d_ext, number(pe, l * 64 + 64))
                for i in range(SUNITS):
                    s_tile(pr, 0, i)
                transpose_max(pr, 0)
                with pe.Fori(0, PAIRS - 1) as p:
                    pair(l, p, False)
                pair(l, PAIRS - 1, True)

            def group_project(pr, rnd):
                pr.wait(gd_wq, 16, 16 * (rnd + 1))
                for j in range(JQ):
                    for ct in range(CT):
                        last = pe.matmul(ST[j][:, :], gwq[:, ct, :], xq[:, ct, j * 512:(j + 1) * 512],
                                         start=ct == 0, stop=ct == CT - 1)
                    last.then_inc(gpe_q, 1)

            def group_s(pr, h, i):
                if i == 0:
                    pr.wait(gd_q, GROUPS * 64, 64 * (h + 1))
                    if h > 0:
                        pr.wait(gdve_mrow, GROUPS, h)
                if i >= 2:
                    pr.wait(gdve_s, GROUPS * SUNITS, h * SUNITS + i - 1)
                elif h > 0:
                    pr.wait(gdve_s, GROUPS * SUNITS, h * SUNITS)
                qt, (o, w) = i // len(KCH), KCH[i % len(KCH)]
                pe.matmul(SS[i % 2][:, 0:w], Q1[h % 2][0:MROW, qt * 128:(qt + 1) * 128], KG[h % GROUPS][0:MROW, o:o + w],
                          start=True, stop=True).then_inc(gpe_s, 1)

            def group_transpose_max(pr, h):
                pr.wait(gdve_m, GROUPS, h + 1)
                pe.transpose(SS[0][0:QT, 0:128], negm[:, :], ident[:, :]).then_inc(gpe_m, 1)

            def group_sums(pr, h):
                pr.wait(gact_o, GROUPS, h + 1)
                if h > 0:
                    pr.wait(gdve_r, GROUPS, h)
                pe.matmul(ZB[:, :], sel[:, :], Oraw[:, h % 2, :], start=True, stop=True).then_inc(gpe_z, 1)

            def group_attend(pr, h, other):
                g = h % GROUPS

                def scores(t, j):
                    k = rows_of(t)
                    if t > 0:
                        pr.wait(gact_p, GROUPS * GUNITS, h * GUNITS + JQ * (t - 1) + j + 1)
                    pe.matmul(ST[j][0:k, :], KG[g][0:MROW + 1, t * 128:t * 128 + k],
                              Q1[h % 2][0:MROW + 1, j * 512:(j + 1) * 512], start=True, stop=True).then_inc(gpe_st, 1)

                pr.wait(gd_m, GROUPS * 16, 16 * (h + 1))
                for j in range(JQ):
                    scores(0, j)
                for t in range(KT):
                    k = rows_of(t)
                    tiles = g_s_units(t) if other else []
                    for j in range(JQ):
                        if t + 1 < KT:
                            scores(t + 1, j)
                        for i in tiles[:1]:
                            group_s(pr, h + 1, i)
                        tiles = tiles[1:]
                    for i in tiles[:1]:
                        group_s(pr, h + 1, i)
                    tiles = tiles[1:]
                    pr.wait(gact_p, GROUPS * GUNITS, h * GUNITS + JQ * (t + 1))
                    if t == 0 and h > 0:
                        group_sums(pr, h - 1)
                    for j in range(JQ):
                        last = pe.matmul(OB[j * QD:j * QD + QD, :], V[0:k, t, g * QD:g * QD + QD],
                                         PG[(t * JQ + j) % len(PG)][0:k, :], start=t == 0, stop=t == KT - 1)
                    last.then_inc(gpe_pv, 1)
                    for i in tiles:
                        group_s(pr, h + 1, i)
                    if other and t == KT - 2:
                        group_transpose_max(pr, h + 1)

            def group_output(pr):
                pr.wait(gd_wo, 16, 16)
                pr.wait(gpool_on, 4 * GROUPS, 4 * GROUPS)
                for i in range(CT * JQ):
                    ct, j = i // JQ, i % JQ
                    if i >= 4:
                        pr.wait(gdve_x, 8, i - 3)
                    pe.matmul(ST[i % 4][:, :], gwo[:, ct * 128:(ct + 1) * 128], On[:, j * 512:(j + 1) * 512],
                              start=True, stop=True).then_inc(gpe_o, 1)
                pr.wait(gdve_x, 8, 8)

            def all_p(pr, h):
                pr.wait(gact_p, GROUPS * GUNITS, (h + 1) * GUNITS)

            def group_layer():
                pe.wait_ge(dve_x, 8 * PAIRS + 1)
                for j in range(JQ):
                    pe.wait_ge(act_sq, j + 1)
                    for ct in range(CT):
                        last = pe.matmul(GB[j][:, :], ones[:, :], P[:, 2 * (j % 2) + ct, :],
                                         start=ct == 0, stop=ct == CT - 1)
                    last.then_inc(pe_sq, 1)
                pe.wait_ge(gd_load, 48)
                for banks, weights, done in ((ST, gwk, gpe_k), (GB, gwv, gpe_v)):
                    for i, (o, w) in enumerate(KCH):
                        if done is gpe_v:
                            pe.wait_ge(dve_var, i + 1)
                            w = min(w, NK - o)
                        for ct in range(CCT):
                            last = pe.matmul(banks[i][:, 0:w], weights[:, ct, :], ctxT[:, ct, o:o + w],
                                             start=ct == 0, stop=ct == CCT - 1)
                        last.then_inc(done, 1)
                pr = Pair(pe, 0, start)
                for i in range(4):
                    pe.wait_ge(gact_vraw, 4)
                    for t in range(4 * i, min(4 * i + 4, KT)):
                        k, c = rows_of(t), t - 4 * i
                        last = pe.transpose(GB[i][0:k, c * 128:(c + 1) * 128], rawV[:, t * 128:t * 128 + k], ident[:, :])
                    last.then_inc(gpe_vt, 1)
                pe.wait_ge(gdve_k, 4)
                pe.wait_ge(g_xq, 1)
                group_project(pr, 0)
                pe.wait_ge(gact_v, 4)
                pe.wait_ge(gd_k, 16 * 4 * GROUPS)
                pe.wait_ge(dve_sel, 4)
                for i in range(SUNITS):
                    group_s(pr, 0, i)
                group_transpose_max(pr, 0)
                group_attend(pr, 0, True)
                with pe.Fori(0, ROUNDS - 1) as r:
                    pr = Pair(pe, r, start)
                    group_attend(pr, 1, True)
                    group_attend(pr, 2, True)
                    all_p(pr, 2)
                    group_project(pr, 1)
                    pr.wait(gdve_q, 4, 8)
                    group_attend(pr, 3, True)
                    group_attend(pr, 4, True)
                    all_p(pr, 4)
                    group_output(pr)
                pr = Pair(pe, ROUNDS - 1, start)
                group_attend(pr, 1, True)
                group_attend(pr, 2, True)
                group_attend(pr, 3, False)
                group_sums(pr, 3)
                all_p(pr, 3)
                group_output(pr)
                pe.wait_ge(gd_bias, 16)

            big_layer(0)
            group_layer()
            with pe.Fori(0, BIG - 1) as l:
                big_layer(pe.snap(l + 1))

            pe.wait_ge(dve_x, BIG * PAIRS * 8 + 1)
            for t in range(QT):
                if t >= 4:
                    pe.wait_ge(dve_out, t - 3)
                for ct in range(CT):
                    last = pe.transpose(ST[t % 4][:, ct * 128:(ct + 1) * 128], xacc[:, ct, t * 128:(t + 1) * 128],
                                        ident[:, :])
                last.then_inc(pe_out, 1)

        @block.scalar
        def _(act):
            act.sem_inc(act_o, 1)

            def copy(out, in_):
                return act.activation(out, in_, ACT.Copy)

            for i in range(QT // 2):
                act.wait_ge(pe_set, i + 1)
                copy(xacc[:, :, 2 * i * 128:(2 * i + 2) * 128].rearrange("p c (t q) -> p c t q", t=2),
                     ST[i % 4][:, :].rearrange("p (t c q) -> p c t q", t=2, c=2)).then_inc(act_set, 1)
            for t in range(KT):
                i = QT // 2 + t
                k = rows_of(t)
                act.wait_ge(pe_set, i + 1)
                copy(ctxT[:, :, t * 128:t * 128 + k],
                     ST[i % 4][:, :].rearrange("p (c k) -> p c k", c=CCT)[:, :, 0:k]).then_inc(act_set, 1)
            copy(ctxT[:, :, NK:KP], ST[(QT // 2 + KT - 1) % 4][:, :].rearrange("p (c k) -> p c k", c=CCT)
                 [:, :, KREST - 1:KREST]).then_inc(act_set, 1)

            def raw_kq(pr, n, which):
                for i in which:
                    pr.wait(pe_kq, 8, 8 * n + i + 1)
                    if i < 4:
                        o, w = KCH[i]
                        copy(rawK[:, o:o + w], ST[i % 4][:, 0:w]).then_inc(act_kq, 1)
                    else:
                        copy(rawQ[:, (i - 4) * 512:(i - 3) * 512], ST[i % 4][:, :]).then_inc(act_kq, 1)

            def hi_k(pr, n, g):
                b = g % 2
                own, other = slice(64 * b, 64 * b + 64), slice(64 * (1 - b), 64 * (1 - b) + 64)
                pr.wait(act_kq, 8, 8 * n + 4)
                for out in (K1[b][own, :], K1[b][other, :], KS[b][own, :]):
                    copy(out, rawK[own, :]).then_inc(act_hi, 1)

            def hi_q(pr, n, g):
                b = g % 2
                own = slice(64 * b, 64 * b + 64)
                pr.wait(act_kq, 8, 8 * n + 8)
                for out in (Q1[b][own, :], Q2[b][own, :]):
                    copy(out, rawQ[own, :]).then_inc(act_hi, 1)

            def raw_v(pr, n):
                for i, (o, w) in enumerate(KCH):
                    w = min(w, NK - o)
                    pr.wait(pe_v, 4, 4 * n + i + 1)
                    copy(rawV[:, o:o + w], ST[i][:, 0:w]).then_inc(act_vraw, 1)

            def tiles_v(pr, n):
                for i in range(4):
                    pr.wait(pe_vt, 4, 4 * n + i + 1)
                    c = min(4, KT - 4 * i)
                    k = rows_of(4 * i + c - 1)
                    copy(V[0:k, 4 * i:4 * i + c, :], ST[i][0:k, 0:c * 128].rearrange("k (t d) -> k t d", d=128))\
                        .then_inc(act_v, 1)

            def take_o(pr, g, c2):
                pr.wait(pe_pv, 2 * STEPS, g * STEPS + (c2 + 1) * KT)
                pr.wait(dve_on, 8, 4 * g)
                copy(Oraw[:, c2, :], OB[:, :]).then_inc(act_o, 1)

            def attend(pr, g):
                for s in range(STEPS):
                    k = rows_of(s % KT)
                    for jj in range(2):
                        u = 2 * s + jj
                        pr.wait(pe_st, 2 * UNITS, g * UNITS + u + 1)
                        v = max(u - NP, -1) + 1
                        pr.wait(pe_pv, 2 * STEPS, g * STEPS + (v + 1) // 2)
                        pr.wait(pool_acc, 2 * UNITS, g * UNITS + v)
                        act.activation(P[0:k, u % NP, :], ST[u % 4][0:k, :], ACT.Exp, scale=SCALE).then_inc(act_p, 1)
                    if s == KT:
                        take_o(pr, g, 0)
                take_o(pr, g, 1)

            def pair(l, p, last):
                pr = Pair(act, number(act, l * PAIRS + p), start)
                attend(pr, 0)
                if not last:
                    pr.wait(dve_lo, 4, 4)
                    raw_kq(pr, 1, range(0, 4))
                    pr.wait(pe_st, 2 * UNITS, UNITS)
                    hi_k(pr, 1, 2)
                    raw_kq(pr, 1, range(4, 8))
                    hi_q(pr, 1, 2)
                attend(pr, 1)
                if not last:
                    pr.wait(pe_st, 2 * UNITS, 2 * UNITS)
                    hi_k(pr, 1, 3)
                    raw_v(pr, 1)
                    hi_q(pr, 1, 3)
                    tiles_v(pr, 1)

            def big_layer(l):
                act.wait_ge(act_set, QT // 2 + KT + 1)
                act.wait_ge(dve_x, number(act, l * (8 * PAIRS) + 1))
                pr = Pair(act, number(act, l * PAIRS), start)
                act.wait_ge(dve_tok, number(act, l * TOK + TOK))
                raw_kq(pr, 0, range(0, 4))
                act.wait_ge(d_ext, number(act, l * 64 + 64))
                hi_k(pr, 0, 0)
                raw_kq(pr, 0, range(4, 8))
                hi_q(pr, 0, 0)
                raw_v(pr, 0)
                tiles_v(pr, 0)
                hi_k(pr, 0, 1)
                hi_q(pr, 0, 1)
                with act.Fori(0, PAIRS - 1) as p:
                    pair(l, p, False)
                pair(l, PAIRS - 1, True)

            def group_hi(pr, rnd):
                for j in range(JQ):
                    pr.wait(gpe_q, 4, 4 * rnd + j + 1)
                    if rnd > 0 and j == 0:
                        pr.wait(gd_q, GROUPS * 64, GROUPS * 64)
                    copy(Q4hi[:, j * 512:(j + 1) * 512], ST[j][:, :]).then_inc(gact_q, 1)

            def group_attend(pr, h):
                for t in range(KT):
                    k = rows_of(t)
                    for j in range(JQ):
                        u = JQ * t + j
                        pr.wait(gpe_st, GROUPS * GUNITS, h * GUNITS + u + 1)
                        if u >= len(PG) or h > 0:
                            v = max(u - len(PG), -1) + 1
                            pr.wait(gpe_pv, GROUPS * KT, h * KT + -(-v // JQ))
                        act.activation(PG[u % len(PG)][0:k, :], ST[j][0:k, :], ACT.Exp, scale=SCALE1)\
                            .then_inc(gact_p, 1)
                pr.wait(gpe_pv, GROUPS * KT, (h + 1) * KT)
                if h > 1:
                    pr.wait(gpool_on, 4 * GROUPS, 4 * (h - 1))
                elif h == 1:
                    pr.wait(gpe_z, GROUPS, 1)
                copy(Oraw[:, h % 2, :], OB[:, :]).then_inc(gact_o, 1)

            def group_layer():
                act.wait_ge(dve_x, 8 * PAIRS + 1)
                for j in range(JQ):
                    if j >= 2:
                        act.wait_ge(pe_sq, j - 1)
                    for ct in range(CT):
                        last = act.activation(P[:, 2 * (j % 2) + ct, :], xacc[:, ct, j * 512:(j + 1) * 512], ACT.Square)
                    last.then_inc(act_sq, 1)
                act.wait_ge(pe_sq, JQ)
                for i, (o, w) in enumerate(KCH):
                    act.wait_ge(gpe_k, i + 1)
                    copy(K4hi[:, o:o + w], ST[i][:, 0:w]).then_inc(gact_k, 1)
                for i, (o, w) in enumerate(KCH):
                    w = min(w, NK - o)
                    act.wait_ge(gpe_v, i + 1)
                    copy(rawV[:, o:o + w], GB[i][:, 0:w]).then_inc(gact_vraw, 1)
                for i in range(4):
                    act.wait_ge(gpe_vt, i + 1)
                    c = min(4, KT - 4 * i)
                    k = rows_of(4 * i + c - 1)
                    copy(V[0:k, 4 * i:4 * i + c, :].rearrange("k t (g d) -> k t g d", g=GROUPS)[:, :, :, 0:D1],
                         GB[i][0:k, 0:c * 128].rearrange("k (t g d) -> k t g d", t=c, g=GROUPS)[:, :, :, 0:D1])\
                        .then_inc(gact_v, 1)
                act.wait_ge(dve_inv, JQ)
                act.activation(On[:, :], On[:, :], ACT.Sqrt).then_inc(act_rms, 1)
                pr = Pair(act, 0, start)
                group_hi(pr, 0)
                act.wait_ge(gd_k, 16 * 4 * GROUPS)
                group_attend(pr, 0)
                with act.Fori(0, ROUNDS - 1) as r:
                    pr = Pair(act, r, start)
                    group_attend(pr, 1)
                    group_attend(pr, 2)
                    group_hi(pr, 1)
                    group_attend(pr, 3)
                    group_attend(pr, 4)
                pr = Pair(act, ROUNDS - 1, start)
                for h in range(1, GROUPS):
                    group_attend(pr, h)
                act.wait_ge(gdve_x, 8 * ROUNDS)

            big_layer(0)
            group_layer()
            with act.Fori(0, BIG - 1) as l:
                big_layer(act.snap(l + 1))

        @block.vector
        def _(dve):
            for s in (dve_s, dve_mrow, dve_r, dve_x, dve_on, dve_m):
                dve.sem_inc(s, 1)
            for b in range(2):
                o = 64 * (1 - b)
                for m in (Q2[b], K2[b], KS[b]):
                    dve.memset(words(m[o:o + 64, :]), 0.0).then_inc(dve_zero, 1)
            dve.wait_ge(d_m, 16)
            m = xq[0:2, 0, :]
            dve.tensor_scalar(m, m, -1.0, 1.0, ALU.mult, ALU.add).then_inc(dve_set, 1)
            dve.wait_ge(dve_set, 1)
            dve.tensor_scalar(m, m, -SUPPRESS / SCALE, None, ALU.mult).then_inc(dve_bias, 1)
            dve.wait_ge(dve_bias, 1)
            dve.tensor_copy(Q1[0][0:2, :], m).then_inc(dve_bias, 1)
            dve.wait_ge(dve_bias, 2)
            dve.tensor_tensor(Q1[1][0:2, :], m, Q1[0][0:2, :], ALU.subtract).then_inc(dve_bias, 1)
            dve.wait_ge(pool_set, 4)
            dve.tensor_scalar(first_row[:, :], tok[:, 7:8].bitcast(I32), 0.0, None, ALU.is_equal).then_inc(dve_set, 1)
            dve.wait_ge(d_biasrow, 128)

            def lo_parts(pr, g):
                b = g % 2
                own, other = slice(64 * b, 64 * b + 64), slice(64 * (1 - b), 64 * (1 - b) + 64)
                pr.wait(act_hi, 10, 5 * (g + 1))
                dve.tensor_tensor(K2[b][own, :], rawK[own, :], K1[b][own, :], ALU.subtract).then_inc(dve_lo, 1)
                dve.tensor_tensor(Q1[b][other, :], rawQ[own, :], Q1[b][own, :], ALU.subtract).then_inc(dve_lo, 1)

            def s_max(pr, g, i):
                w = KCH[i % len(KCH)][1]
                if i == 0:
                    pr.wait(dve_m, 2, g)
                pr.wait(pe_s, 2 * SUNITS, g * SUNITS + i + 1)
                dve.tensor_reduce(mpart[:, i // len(KCH), i % len(KCH):i % len(KCH) + 1], SS[i % 2][:, 0:w],
                                  AX.X, ALU.max).then_inc(dve_s, 1)

            def head_max(pr, g):
                pr.wait(dve_s, 2 * SUNITS, (g + 1) * SUNITS)
                dve.tensor_reduce(negm[:, :], mpart[:, :, :], AX.X, ALU.max, negate=True).then_inc(dve_m, 1)

            def max_row(pr, g):
                pr.wait(pe_m, 2, g + 1)
                pr.wait(d_m, 32, 16 * g)
                dve.tensor_copy(mrow[:, :], SS[0][0:QT, 0:128]).then_inc(dve_mrow, 1)

            def reciprocals(pr, g, c2, piece):
                q = slice(piece * 128, piece * 128 + 128)
                if piece == 0:
                    pr.wait(dve_on, 8, 4 * g + 2 * c2)
                    pr.wait(pe_z, 4, 2 * g + c2 + 1)
                ins = dve.reciprocal(R[:, q], ZB[:, q])
                if piece == 3:
                    ins.then_inc(dve_r, 1)

            def divide(pr, g, c2):
                b = g % 2
                pr.wait(dve_r, 4, 2 * g + c2 + 1)
                pr.wait(act_o, 4, 2 * g + c2 + 1)
                if g == 0 and c2 == 0:
                    pr.wait(pe_o, 8, 0)
                for jj in range(2):
                    j, r = 2 * c2 + jj, slice(64 * jj, 64 * jj + 64)
                    dve.tensor_tensor(On[64 * b:64 * b + 64, j * 512:(j + 1) * 512], Oraw[r, c2, :], R[r, :],
                                      ALU.mult).then_inc(dve_on, 1)

            def normalise(pr, g, c2):
                for piece in range(4):
                    reciprocals(pr, g, c2, piece)
                divide(pr, g, c2)

            def attend(pr, g, other):
                for s in range(STEPS):
                    if other is not None:
                        for i in s_units(s):
                            s_max(pr, other, i)
                    if KT + 4 <= s < KT + 8:
                        reciprocals(pr, g, 0, s - KT - 4)
                    if s == KT + 8:
                        divide(pr, g, 0)

            def add_output(pr):
                for i in range(CT * JQ):
                    ct, j = i // JQ, i % JQ
                    pr.wait(pe_o, 8, i + 1)
                    x = xacc[:, ct, j * 512:(j + 1) * 512]
                    dve.tensor_tensor(x, ST[i % 4][:, :], x, ALU.add).then_inc(dve_x, 1)

            def pair(l, p, last):
                pr = Pair(dve, number(dve, l * PAIRS + p), start)
                attend(pr, 0, 1)
                head_max(pr, 1)
                max_row(pr, 1)
                normalise(pr, 0, 1)
                if not last:
                    lo_parts(pr, 2)
                attend(pr, 1, None if last else 2)
                if not last:
                    head_max(pr, 2)
                    max_row(pr, 2)
                normalise(pr, 1, 1)
                if not last:
                    lo_parts(pr, 3)
                add_output(pr)

            dve.wait_ge(act_set, QT // 2 + KT + 1)
            def big_layer(l):
                dve.wait_ge(d_layer, number(dve, l * 48 + 48))
                steps = number(dve, l * TOK)

                def link(ins, k):
                    ins.then_inc(dve_tok, 1)
                    dve.wait_ge(dve_tok, steps + k)
                key, hit, hit2 = rawK[0:NROWS, :], rawQ[0:NROWS, 0:KP], On[0:NROWS, 0:KP]
                link(dve.tensor_copy(tok[:, 0:4], tok_i[:, :]), 1)
                link(dve.tensor_scalar(R[0:NROWS, 0:4], tok[:, 0:4], 0.0, float(NK), ALU.is_lt, ALU.mult), 2)
                link(dve.tensor_tensor(tok[:, 0:4], tok[:, 0:4], R[0:NROWS, 0:4], ALU.add), 3)
                link(dve.tensor_scalar(hit, key, tok[:, 2:3], None, ALU.is_equal), 4)
                link(dve.scalar_tensor_tensor(hit, key, tok[:, 3:4], hit, ALU.is_equal, ALU.max), 5)
                link(dve.tensor_scalar(hit, hit, -1.0, 1.0, ALU.mult, ALU.add), 6)
                link(dve.tensor_scalar(hit2, key, tok[:, 0:1], None, ALU.is_equal), 7)
                link(dve.scalar_tensor_tensor(hit2, key, tok[:, 1:2], hit2, ALU.is_equal, ALU.max), 8)
                link(dve.tensor_tensor(hit2, hit2, hit, ALU.mult), 9)
                link(dve.tensor_scalar(K1[1][0:NROWS, :], hit2, first_row[:, 0:1], None, ALU.add), TOK)
                dve.tensor_copy(xq[:, :, :], xacc[:, :, :]).then_inc(dve_xq, 1)
                dve.wait_ge(dve_xq, number(dve, l + 1))
                for ct in range(CT):
                    last = dve.tensor_scalar(xacc[:, ct, :], xacc[:, ct, :], bo[:, ct:ct + 1], None, ALU.add)
                last.then_inc(dve_bo, 1)
                dve.wait_ge(dve_bo, number(dve, l + 1))
                pr = Pair(dve, number(dve, l * PAIRS), start)
                lo_parts(pr, 0)
                for i in range(SUNITS):
                    s_max(pr, 0, i)
                head_max(pr, 0)
                max_row(pr, 0)
                lo_parts(pr, 1)
                with dve.Fori(0, PAIRS - 1) as p:
                    pair(l, p, False)
                pair(l, PAIRS - 1, True)

            def group_lo(pr, rnd):
                for j in range(JQ):
                    q = slice(j * 512, (j + 1) * 512)
                    pr.wait(gact_q, 4, 4 * rnd + j + 1)
                    dve.tensor_tensor(Q4lo[:, q], ST[j][:, :], Q4hi[:, q], ALU.subtract).then_inc(gdve_q, 1)

            def group_s_max(pr, h, i):
                w = KCH[i % len(KCH)][1]
                if i == 0 and h > 0:
                    pr.wait(gdve_m, GROUPS, h)
                pr.wait(gpe_s, GROUPS * SUNITS, h * SUNITS + i + 1)
                dve.tensor_reduce(mpart[:, i // len(KCH), i % len(KCH):i % len(KCH) + 1], SS[i % 2][:, 0:w],
                                  AX.X, ALU.max).then_inc(gdve_s, 1)

            def group_max(pr, h):
                pr.wait(gdve_s, GROUPS * SUNITS, (h + 1) * SUNITS)
                dve.tensor_reduce(negm[:, :], mpart[:, :, :], AX.X, ALU.max, negate=True).then_inc(gdve_m, 1)
                pr.wait(gpe_m, GROUPS, h + 1)
                if h > 0:
                    pr.wait(gd_m, 16 * GROUPS, 16 * h)
                dve.tensor_copy(mrow[:, :], SS[0][0:QT, 0:128]).then_inc(gdve_mrow, 1)

            def group_reciprocals(pr, h, piece):
                q = slice(piece * 128, piece * 128 + 128)
                if piece == 0:
                    pr.wait(gpe_z, GROUPS, h + 1)
                    if h > 0:
                        pr.wait(gpool_on, 4 * GROUPS, 4 * h)
                ins = dve.reciprocal(R[:, q], ZB[:, q])
                if piece == 3:
                    ins.then_inc(gdve_r, 1)

            def group_attend(pr, h, other):
                for t in range(KT):
                    for i in g_s_units(t) if other else []:
                        group_s_max(pr, h + 1, i)
                    if h > 0 and t < 4:
                        group_reciprocals(pr, h - 1, t)
                if other:
                    group_max(pr, h + 1)

            def group_add(pr):
                for i in range(CT * JQ):
                    ct, j = i // JQ, i % JQ
                    pr.wait(gpe_o, 8, i + 1)
                    x = xacc[:, ct, j * 512:(j + 1) * 512]
                    dve.tensor_tensor(x, ST[i % 4][:, :], x, ALU.add).then_inc(gdve_x, 1)

            def group_layer():
                for j in range(GROUPS):
                    dve.tensor_scalar(sel[:, j * QD:(j + 1) * QD], ones[:, 0:QD], ident[:, j * QD + D1:j * QD + D1 + 1],
                                      None, ALU.mult).then_inc(dve_sel, 1)
                for j in range(JQ):
                    dve.wait_ge(pe_sq, j + 1)
                    dve.tensor_scalar(rawQ[:, j * 512:(j + 1) * 512], GB[j][:, :], 1.0 / C, EPS, ALU.mult, ALU.add)\
                        .then_inc(dve_var, 1)
                for j in range(JQ):
                    q = slice(j * 512, (j + 1) * 512)
                    dve.wait_ge(dve_var, j + 1)
                    dve.reciprocal(On[:, q], rawQ[:, q]).then_inc(dve_inv, 1)
                    o, w = KCH[j]
                    dve.wait_ge(gact_k, j + 1)
                    dve.tensor_tensor(K4lo[:, o:o + w], ST[j][:, 0:w], K4hi[:, o:o + w], ALU.subtract).then_inc(gdve_k, 1)
                dve.wait_ge(act_rms, 1)
                dve.wait_ge(gd_load, 48)
                for ct in range(CT):
                    last = dve.scalar_tensor_tensor(xq[:, ct, :], xacc[:, ct, :], nw[:, ct:ct + 1], On[:, :],
                                                    ALU.mult, ALU.mult)
                last.then_inc(g_xq, 1)
                pr = Pair(dve, 0, start)
                group_lo(pr, 0)
                for i in range(SUNITS):
                    group_s_max(pr, 0, i)
                group_max(pr, 0)
                group_attend(pr, 0, True)
                with dve.Fori(0, ROUNDS - 1) as r:
                    pr = Pair(dve, r, start)
                    group_attend(pr, 1, True)
                    group_attend(pr, 2, True)
                    group_lo(pr, 1)
                    group_attend(pr, 3, True)
                    group_attend(pr, 4, True)
                    group_add(pr)
                pr = Pair(dve, ROUNDS - 1, start)
                for h in range(1, GROUPS):
                    group_attend(pr, h, h < GROUPS - 1)
                for piece in range(4):
                    group_reciprocals(pr, GROUPS - 1, piece)
                group_add(pr)
                dve.wait_ge(gdve_x, 8 * ROUNDS)

            big_layer(0)
            group_layer()
            with dve.Fori(0, BIG - 1) as l:
                big_layer(dve.snap(l + 1))

            for t in range(QT):
                dve.wait_ge(pe_out, t + 1)
                dve.tensor_copy(x_out[:, t, :], ST[t % 4][:, 0:C]).then_inc(dve_out, 1)


def kernel(**inp):
    import concourse.bacc as bacc
    from concourse.bass_utils import run_bass_kernel_spmd as run

    big = ["L0_xattn_", "L2_xattn_", "L3_xattn_"]
    f = np.float32
    wq = np.zeros((BIG, C, HEADS, D), f)
    wk = np.zeros((BIG, CC, HEADS, D), f)
    wv = np.zeros((BIG, CC, HEADS, D), f)
    wo = np.zeros((BIG, HEADS, D, C), f)
    bo = np.zeros((BIG, C), f)
    tok = np.full((BIG, NROWS, 4), NONE, np.int32)
    for l, k in enumerate(big):
        wq[l] = np.asarray(inp[k + "Wq"]).reshape(C, HEADS, D)
        wk[l] = np.asarray(inp[k + "Wk"]).reshape(CC, HEADS, D)
        wv[l] = np.asarray(inp[k + "Wv"]).reshape(CC, HEADS, D)
        wo[l] = np.asarray(inp[k + "Wo"]).reshape(HEADS, D, C)
        bo[l] = np.asarray(inp[k + "bo"])
        A, B = np.asarray(inp[k + "token_indices_A"]), np.asarray(inp[k + "token_indices_B"])
        tok[l, 1:3, 0:2] = A
        tok[l, 1:3, 2:4] = B
        tok[l, 3:5, 0:2] = B

    def quadrants(w):
        out = np.zeros((w.shape[0], GROUPS, QD), f)
        out[:, :, :D1] = w
        return np.ascontiguousarray(out.reshape(-1, P128, GROUPS * QD).transpose(1, 0, 2))

    gq = np.asarray(inp["L1_xattn_wq"]).reshape(C, GROUPS, ROUNDS, D1)
    gwq = np.stack([quadrants(gq[:, :, r]) for r in range(ROUNDS)] + [quadrants(gq[:, :, 0])])
    gwo = np.zeros((ROUNDS, GROUPS, QD, C), f)
    gwo[:, :, :D1] = np.asarray(inp["L1_xattn_wo"]).reshape(GROUPS, ROUNDS, D1, C).transpose(1, 0, 2, 3)

    def columns(w, n):
        w = w.reshape(BIG, n, P128, PAIRS, 2 * D).transpose(0, 3, 2, 1, 4).reshape(BIG * PAIRS, P128, n, 2 * D)
        return np.ascontiguousarray(np.concatenate([w, w[:1]]))

    def vectors(v):
        return np.ascontiguousarray(v.reshape(BIG, CT, P128).transpose(0, 2, 1))

    wo = wo.reshape(BIG * PAIRS, 2 * D, C)
    arrays = {
        "x": np.ascontiguousarray(np.asarray(inp["x"])[0]),
        "ctx": np.ascontiguousarray(np.asarray(inp["ctx_2048"])[0]),
        "mask": np.stack([np.asarray(inp["mask_S_fk1"]), np.asarray(inp["mask_S_fk0"])]),
        "wq": columns(wq, CT), "wk": columns(wk, CCT), "wv": columns(wv, CCT),
        "wo": np.ascontiguousarray(np.concatenate([wo, wo[:1]])),
        "bo": vectors(bo), "tok": tok,
        "gwk": quadrants(np.asarray(inp["L1_xattn_wk"]).reshape(CC, GROUPS, D1)),
        "gwv": quadrants(np.asarray(inp["L1_xattn_wv"]).reshape(CC, GROUPS, D1)),
        "gwq": gwq, "gwo": gwo.reshape(ROUNDS, P128, C),
        "nw": np.ascontiguousarray(np.asarray(inp["L1_xattn_norm_w"]).reshape(CT, P128).T),
        "key": np.tile(np.minimum(np.arange(KP), NK - 1).astype(f), (NROWS, 1)),
    }
    nc = bacc.Bacc("TRN2", target_bir_lowering=False, num_devices=1)
    aps = {k: nc.dram_tensor(f"in_{k}", v.shape, mybir.dt.from_np(v.dtype), kind="ExternalInput").ap()
           for k, v in arrays.items()}
    aps["out"] = nc.dram_tensor("out", (NQ, C), F32, kind="ExternalOutput").ap()
    attention_layers(nc, aps)
    r = run(nc, [{f"in_{k}": v for k, v in arrays.items()}], core_ids=[0])
    return r.results[0]["out"].reshape(1, NQ, C)
```

```python
from contextlib import ExitStack

import numpy as np
import concourse.bass as bass
from concourse import mybir
from concourse.alu_op_type import AluOpType as ALU

F32 = mybir.dt.float32
F32R = mybir.dt.float32r
I32 = mybir.dt.int32
ACT = mybir.ActivationFunctionType
AX = mybir.AxisListType

P128 = 128
BIG, HEADS, D = 3, 16, 64
GROUPS, D1 = 4, 16
ROUNDS = HEADS // GROUPS
NQ, NK, C, CC = 2048, 1601, 256, 512
PAIRS = HEADS // 2
QT, KT = NQ // P128, -(-NK // P128)
KREST = NK - (KT - 1) * P128
KP = NK + 1
KCH = [(0, 402), (402, 400), (802, 400), (1202, 400)]
TOK = 10
JQ = NQ // 512
CT, CCT = C // P128, CC // P128
NP = 6
STEPS = 2 * KT
UNITS = 2 * STEPS
SUNITS = QT * len(KCH)
SUPPRESS, SCALE, EPS = 20.0, 0.125, 1e-5
NROWS = 5
NONE = 4096
SCALE1 = D1 ** -0.5
QD = 32
MROW = 3 * QD + D1
GUNITS = KT * JQ
GSTEPS = range(0, KT - 2)


def s_units(step):
    first, steps = 2, STEPS - 2
    if not first <= step < first + steps:
        return range(0)
    a, b = step - first, step - first + 1
    return range(a * SUNITS // steps, b * SUNITS // steps)


def adds(alone):
    owner = {}
    for u in range(UNITS):
        t, jj = u // 2 % KT, u % 2
        if t > 0:
            owner[u] = "dve" if jj == 1 and t >= 2 and (alone or t % 4 == 0) else "pool"
    at = {u: UNITS if u == max(v for v in owner if owner[v] == e) else u + 1 for u, e in owner.items()}
    return owner, at


def g_s_units(t):
    if t not in GSTEPS:
        return []
    a = t - GSTEPS.start
    return list(range(a * SUNITS // len(GSTEPS), (a + 1) * SUNITS // len(GSTEPS)))


def number(eng, v):
    return v if isinstance(v, int) else eng.snap(v)


def words(ap):
    return ap.bitcast(F32)


def rows_of(t):
    return KREST if t == KT - 1 else P128


class Pair:

    def __init__(self, eng, n, start, ahead=()):
        self.eng, self.n, self.start, self.made = eng, n, start, {}
        self.ahead = {(m, c): number(eng, n * m + c) for m, c in ahead}

    def wait(self, sem, per_pair, plus):
        plus += self.start.get(sem.name, 0)
        if (per_pair, plus) in self.ahead:
            self.eng.wait_ge(sem, self.ahead[per_pair, plus])
            return
        if per_pair not in self.made:
            self.made[per_pair] = number(self.eng, self.n * per_pair)
        self.eng.wait_ge(sem, self.made[per_pair] + plus)


def attention_layers(nc, a):
    with ExitStack() as ctx:
        def sb(name, shape, dt=F32):
            return ctx.enter_context(nc.sbuf_tensor(name, shape, dt))

        start = {}

        def sem(name):
            return ctx.enter_context(nc.semaphore(name))

        def from_one(name):
            start[name] = 1
            return sem(name)

        ctxT = sb("ctxT", [128, CCT, KP])
        xacc = sb("xacc", [128, CT, NQ])
        xq = sb("xq", [128, CT, NQ])
        ident = sb("ident", [128, 128])
        ones = sb("ones", [128, 128])
        wk = sb("wk", [128, CCT, 128])
        wv = sb("wv", [128, CCT, 128])
        wq = sb("wq", [128, CT, 128])
        wo = sb("wo", [128, C])
        rawK = sb("rawK", [128, KP])
        rawQ = sb("rawQ", [128, NQ])
        rawV = sb("rawV", [128, NK])
        V = sb("V", [128, KT, 128])
        Q1 = [sb(f"Q1_{b}", [128, NQ], F32R) for b in range(2)]
        Q2 = [sb(f"Q2_{b}", [128, NQ], F32R) for b in range(2)]
        K1 = [sb(f"K1_{b}", [128, KP], F32R) for b in range(2)]
        K2 = [sb(f"K2_{b}", [128, KP], F32R) for b in range(2)]
        KS = [sb(f"KS_{b}", [128, KP], F32R) for b in range(2)]
        P = sb("P", [128, NP, 512])
        acc = sb("acc", [128, 2, 2, 512])
        Oraw = sb("Oraw", [128, 2, 512])
        R = sb("R", [128, 512])
        On = sb("On", [128, NQ])
        mpart = sb("mpart", [128, QT, len(KCH)])
        negm = sb("negm", [128, QT])
        mrow = sb("mrow", [QT, 128], F32R)
        tok_i = sb("tok_i", [NROWS, 4], I32)
        tok = sb("tok", [NROWS, 8])
        first_row = sb("first_row", [NROWS, 1])
        nw = sb("nw", [128, CT])
        bo = sb("bo", [128, CT])
        sel = sb("sel", [128, 128])
        KG = [K1[0], K1[1], K2[0], K2[1]]
        gwk, gwv = (rawK[:, i * CCT * 128:(i + 1) * CCT * 128].rearrange("p (t m) -> p t m", m=128) for i in range(2))
        gwq = rawK[:, 2 * CCT * 128:(2 * CCT + CT) * 128].rearrange("p (t m) -> p t m", m=128)
        gwo = rawK[:, (2 * CCT + CT) * 128:(2 * CCT + CT) * 128 + C]
        K4hi = P[:, :, :].rearrange("p n q -> p (n q)")[:, 0:KP].bitcast(F32R)
        K4lo = acc[:, :, :, :].rearrange("p a b q -> p (a b q)")[:, 0:KP].bitcast(F32R)
        Q4hi, Q4lo = Q2[0], rawQ[:, :].bitcast(F32R)
        PG = [P[:, i, :] for i in range(NP)] + [acc[:, i // 2, i % 2, :] for i in range(3)]
        Z = acc[:, 1, 1, :]

        ST = [ctx.enter_context(nc.psum_tensor(f"ST{i}", [128, 512], F32)) for i in range(4)]
        SS = [ctx.enter_context(nc.psum_tensor(f"SS{i}", [128, 512], F32)) for i in range(2)]
        OB = ctx.enter_context(nc.psum_tensor("OB", [128, 512], F32))
        ZB = ctx.enter_context(nc.psum_tensor("ZB", [128, 512], F32))
        GB = [SS[0], SS[1], OB, ZB]
        GS = [SS[0], SS[1], ZB]

        d_x, d_in = sem("d_x"), sem("d_in")
        d_biasrow = sem("d_biasrow")
        d_layer = sem("d_layer")
        d_ext = sem("d_ext")
        d_out = sem("d_out")
        pool_set = sem("pool_set")
        pe_set = sem("pe_set")
        act_set = sem("act_set")
        dve_set = sem("dve_set")
        dve_zero = sem("dve_zero")
        dve_bias = sem("dve_bias")
        dve_tok = sem("dve_tok")
        dve_xq = sem("dve_xq")
        dve_bo = sem("dve_bo")
        pe_out = sem("pe_out")
        dve_out = sem("dve_out")
        d_wkq, d_wv, d_wo = sem("d_wkq"), sem("d_wv"), sem("d_wo")
        pe_kq = sem("pe_kq")
        act_kq = sem("act_kq")
        pe_v = sem("pe_v")
        act_vraw = sem("act_vraw")
        pe_vt = sem("pe_vt")
        act_v = sem("act_v")
        pe_o = from_one("pe_o")
        dve_x = sem("dve_x")
        act_hi = sem("act_hi")
        d_hi = [sem("d_hi_even"), sem("d_hi_odd")]
        dve_lo = sem("dve_lo")
        pe_s = sem("pe_s")
        dve_s = from_one("dve_s")
        dve_m = from_one("dve_m")
        pe_m = sem("pe_m")
        dve_mrow = from_one("dve_mrow")
        d_m = sem("d_m")
        pe_st = from_one("pe_st")
        act_p = sem("act_p")
        pool_acc = from_one("pool_acc")
        dve_acc = from_one("dve_acc")
        acc_sem = {"pool": pool_acc, "dve": dve_acc}
        pe_pv = from_one("pe_pv")
        act_o = from_one("act_o")
        pe_z = from_one("pe_z")
        dve_r = from_one("dve_r")
        dve_on = from_one("dve_on")

        start["d_m"] = 16
        start["dve_x"] = 4

        gd_load = sem("gd_load")
        gd_k = sem("gd_k")
        act_sq, pe_sq, dve_var = sem("act_sq"), sem("pe_sq"), sem("dve_var")
        dve_inv, act_rms, g_xq = sem("dve_inv"), sem("act_rms"), sem("g_xq")
        pool_ones = sem("pool_ones")
        dve_sel = sem("dve_sel")
        gpe_k, gact_k, gdve_k = sem("gpe_k"), sem("gact_k"), sem("gdve_k")
        gpe_v, gact_vraw, gpe_vt, gact_v = sem("gpe_v"), sem("gact_vraw"), sem("gpe_vt"), sem("gact_v")
        pool_clear = sem("pool_clear")
        gd_bias = sem("gd_bias")
        gd_wq, gd_wo = sem("gd_wq"), sem("gd_wo")
        gpe_q, gact_q, gdve_q = sem("gpe_q"), sem("gact_q"), sem("gdve_q")
        gpe_o, gdve_x = sem("gpe_o"), sem("gdve_x")
        gd_q = sem("gd_q")
        gpe_s, gdve_s = sem("gpe_s"), sem("gdve_s")
        gdve_m, gpe_m, gdve_mrow = sem("gdve_m"), sem("gpe_m"), sem("gdve_mrow")
        gd_m = sem("gd_m")
        gpe_st, gact_p = sem("gpe_st"), sem("gact_p")
        gpe_pv = sem("gpe_pv")
        gact_o, gpe_z = sem("gact_o"), sem("gpe_z")
        gact_z, gdve_r = sem("gact_z"), sem("gdve_r")
        gpool_on = sem("gpool_on")

        def add_unit(eng, name, pr, g, u, alone):
            owner, at = adds(alone)
            if owner.get(u) != name:
                return
            t, out, done = u // 2 % KT, acc[0:rows_of(u // 2 % KT), u // (2 * KT), u % 2, :], acc_sem[name]
            raised = at[u] - max([at[v] for v in owner if owner[v] == name and v < u], default=0)
            pr.wait(act_p, 2 * UNITS, g * UNITS + u + 1)
            if t == 1:
                pr.wait(pe_z, 4, 2 * g)
                eng.tensor_tensor(out, P[:, (u - 2) % NP, :], P[:, u % NP, :], ALU.add).then_inc(done, raised)
            else:
                pr.wait(acc_sem[owner[u - 2]], 2 * UNITS, g * UNITS + at[u - 2])
                eng.tensor_tensor(out, out, P[0:rows_of(t), u % NP, :], ALU.add).then_inc(done, raised)

        def wait_added(pr, g, u, alone):
            owner, at = adds(alone)
            u = u + 2 if u // 2 % KT == 0 else u
            pr.wait(acc_sem[owner[u]], 2 * UNITS, g * UNITS + at[u])

        block = ctx.enter_context(nc.Block())

        x_land = [rawQ[:, :].rearrange("p (t c) -> p t c", c=C), On[:, :].rearrange("p (t c) -> p t c", c=C)]
        ctx_land = [P[:, i, :] for i in range(6)] + [acc[:, i // 2, i % 2, :] for i in range(4)] \
            + [Oraw[:, i, :] for i in range(2)] + [R[0:KREST, :]]
        XH = QT // 2
        x_out = xq[:, :, :].rearrange("p a b -> p (a b)").rearrange("p (t c) -> p t c", c=C)

        @block.sync
        def _(sp):
            for i in range(2):
                sp.dma_start(x_land[i], a["x"][i * XH * 128:(i + 1) * XH * 128, :]
                             .rearrange("(t p) c -> p t c", p=128)).then_inc(d_x, 16)
            sp.dma_start(P[:, :, :], a["ctx"][0:768, :].rearrange("(t p) c -> p t c", p=128)).then_inc(d_in, 16)
            sp.dma_start(acc[:, :, :, :].rearrange("p a b c -> p (a b) c"),
                         a["ctx"][768:1280, :].rearrange("(t p) c -> p t c", p=128)).then_inc(d_in, 16)
            sp.dma_start(Oraw[:, :, :], a["ctx"][1280:1536, :].rearrange("(t p) c -> p t c", p=128)).then_inc(d_in, 16)
            sp.dma_start(R[0:KREST, :], a["ctx"][1536:NK, :]).then_inc(d_in, 16)
            sp.dma_start(xq[0:2, 0, :], a["mask"][:, :]).then_inc(d_m, 16)
            sp.dma_start(wk[:, :, :], a["wk"][0, :, :, :]).then_inc(d_wkq, 16)
            sp.dma_start(wq[:, :, :], a["wq"][0, :, :, :]).then_inc(d_wkq, 16)
            sp.dma_start(wv[:, :, :], a["wv"][0, :, :, :]).then_inc(d_wv, 16)
            sp.dma_start(wo[:, :], a["wo"][0, :, :]).then_inc(d_wo, 16)
            sp.wait_ge(dve_bias, 3)
            sp.wait_ge(dve_zero, 6)
            for b in range(2):
                o = 64 * (1 - b)
                for r in range(4):
                    sp.dma_start(words(Q2[b][o + 1 + r:o + 2 + r, :]), words(Q1[r % 2][r // 2:r // 2 + 1, :])).then_inc(d_biasrow, 16)
            sp.wait_ge(d_biasrow, 128)

            def load_kq(n):
                sp.dma_start(wk[:, :, :], a["wk"][n, :, :, :]).then_inc(d_wkq, 16)
                sp.dma_start(wq[:, :, :], a["wq"][n, :, :, :]).then_inc(d_wkq, 16)

            def max_row(b, pr, g):
                pr.wait(dve_mrow, 2, g + 1)
                o = 64 * (1 - b)
                sp.dma_start(words(Q2[b][o:o + 1, :]).rearrange("o (t p) -> o t p", p=128), words(mrow[:, :])).then_inc(d_m, 16)

            def copy_hi(pr, g):
                b = g % 2
                own, other = slice(64 * b, 64 * b + 64), slice(64 * (1 - b), 64 * (1 - b) + 64)
                pr.wait(act_hi, 4, 2 * g + 1)
                sp.dma_start(words(KS[b][own, :]), words(K1[b][own, :])).then_inc(d_hi[b], 16)
                sp.dma_start(words(K1[b][other, :]), words(K1[b][own, :])).then_inc(d_hi[b], 16)
                pr.wait(act_hi, 4, 2 * g + 2)
                sp.dma_start(words(Q2[b][own, :]), words(Q1[b][own, :])).then_inc(d_hi[b], 16)

            def pair(l, p, last):
                n = number(sp, l * PAIRS + p)
                n1, n2 = number(sp, n + 1), number(sp, n + 2)
                pr = Pair(sp, n, start, [(2, 3), (8, 9)] + ([] if last else [(8, 16), (2, 4), (4, 8)]))
                max_row(1, pr, 1)
                if not last:
                    copy_hi(pr, 2)
                    pr.wait(pe_kq, 8, 16)
                    load_kq(n2)
                    max_row(0, pr, 2)
                    copy_hi(pr, 3)
                    pr.wait(pe_v, 4, 8)
                    sp.dma_start(wv[:, :, :], a["wv"][n2, :, :, :]).then_inc(d_wv, 16)
                pr.wait(pe_o, 8, 8)
                sp.dma_start(wo[:, :], a["wo"][n1, :, :]).then_inc(d_wo, 16)

            def big_layer(l):
                n0 = number(sp, l * PAIRS)
                n1 = number(sp, n0 + 1)
                written, rows_made = number(sp, l * (8 * PAIRS) + 1), number(sp, l * TOK + TOK)
                pr = Pair(sp, n0, start, [(8, 8), (4, 4), (2, 2)])
                sp.wait_ge(pe_o, written)
                sp.dma_start(rawK[0:NROWS, :], a["key"][:, :]).then_inc(d_layer, 16)
                sp.dma_start(tok_i[:, :], a["tok"][l, :, :]).then_inc(d_layer, 16)
                sp.dma_start(bo[:, :], a["bo"][l, :, :]).then_inc(d_layer, 16)
                sp.wait_ge(dve_tok, rows_made)
                for b in range(2):
                    o = 64 * (1 - b)
                    sp.dma_start(words(K2[b][o:o + NROWS, :]), words(K1[1][0:NROWS, :])).then_inc(d_ext, 16)
                    sp.dma_start(words(KS[b][o + 1:o + NROWS, :]), words(K1[1][1:NROWS, :])).then_inc(d_ext, 16)
                copy_hi(pr, 0)
                pr.wait(pe_kq, 8, 8)
                load_kq(n1)
                pr.wait(pe_v, 4, 4)
                sp.dma_start(wv[:, :, :], a["wv"][n1, :, :, :]).then_inc(d_wv, 16)
                copy_hi(pr, 1)
                max_row(0, pr, 0)
                with sp.Fori(0, PAIRS - 1) as p:
                    pair(l, p, False)
                pair(l, PAIRS - 1, True)

            def stack(to, hi, lo, order, done):
                for i, part in enumerate(order):
                    rows = QD if i < 3 else D1
                    src = (hi, lo)[part]
                    sp.dma_start(words(to[i * QD:i * QD + rows, :]), src[0:rows, :]).then_inc(done, 16)

            def group_q(pr, h):
                g = h % GROUPS
                if g == 0:
                    pr.wait(gdve_q, 4, 4 * (h // GROUPS + 1))
                elif h >= 2:
                    pr.wait(gpe_st, GROUPS * GUNITS, (h - 1) * GUNITS)
                q = slice(g * QD, g * QD + QD)
                stack(Q1[h % 2], words(Q4hi[q, :]), words(Q4lo[q, :]), (0, 1, 0, 1), gd_q)

            def group_max(pr, h):
                pr.wait(gdve_mrow, GROUPS, h + 1)
                sp.dma_start(words(Q1[h % 2][MROW:MROW + 1, :]).rearrange("o (t p) -> o t p", p=128),
                             words(mrow[:, :])).then_inc(gd_m, 16)

            def group_layer():
                sp.wait_ge(dve_x, 8 * PAIRS + start["dve_x"])
                sp.dma_start(gwk, a["gwk"][:, :, :]).then_inc(gd_load, 16)
                sp.dma_start(gwv, a["gwv"][:, :, :]).then_inc(gd_load, 16)
                sp.dma_start(nw[:, :], a["nw"][:, :]).then_inc(gd_load, 16)
                sp.dma_start(gwq, a["gwq"][0, :, :, :]).then_inc(gd_wq, 16)
                sp.dma_start(gwo, a["gwo"][0, :, :]).then_inc(gd_wo, 16)
                sp.wait_ge(pool_ones, GROUPS + 1)
                sp.wait_ge(gdve_k, 4)
                for g in range(GROUPS):
                    k = slice(g * QD, g * QD + QD)
                    stack(KG[g], words(K4hi[k, :]), words(K4lo[k, :]), (0, 0, 1, 1), gd_k)
                pr = Pair(sp, 0, start)
                group_q(pr, 0)
                sp.dma_start(gwq, a["gwq"][1, :, :, :]).then_inc(gd_wq, 16)
                group_max(pr, 0)
                group_q(pr, 1)
                group_max(pr, 1)
                with sp.Fori(0, ROUNDS - 1) as r:
                    r1, r2 = sp.snap(r + 1), sp.snap(r + 2)
                    heads = range(2, 2 + GROUPS)
                    pr = Pair(sp, r, start, [(GROUPS * GUNITS, (h - 1) * GUNITS) for h in heads]
                              + [(GROUPS, h + 1) for h in heads] + [(4, 8), (8, 8)])
                    for h in heads:
                        group_q(pr, h)
                        if h == GROUPS:
                            sp.dma_start(gwq, a["gwq"][r2, :, :, :]).then_inc(gd_wq, 16)
                        group_max(pr, h)
                    pr.wait(gpe_o, 8, 8)
                    sp.dma_start(gwo, a["gwo"][r1, :, :]).then_inc(gd_wo, 16)
                pr = Pair(sp, ROUNDS - 1, start)
                for h in range(2, GROUPS):
                    group_q(pr, h)
                    group_max(pr, h)
                sp.wait_ge(pool_clear, 3)
                sp.dma_start(words(Q2[0][64 + 1:64 + NROWS, :]), words(Q2[1][1:NROWS, :])).then_inc(gd_bias, 16)
                sp.wait_ge(gd_bias, 16)

            big_layer(0)
            group_layer()
            with sp.Fori(0, BIG - 1) as l:
                big_layer(sp.snap(l + 1))

            for t in range(0, QT, 4):
                sp.wait_ge(dve_out, t + 4)
                sp.dma_start(a["out"][t * 128:(t + 4) * 128, :].rearrange("(t p) c -> p t c", p=128),
                             x_out[:, t:t + 4, :]).then_inc(d_out, 16)
            sp.wait_ge(d_out, 16 * QT // 4)
            sp.wait_ge(d_wkq, 32 * (BIG * PAIRS + 1))
            sp.wait_ge(d_wv, 16 * (BIG * PAIRS + 1))
            sp.wait_ge(d_wo, 16 * (BIG * PAIRS + 1))
            sp.wait_ge(gd_wq, 16 * (ROUNDS + 1))

        @block.gpsimd
        def _(gp):
            gp.sem_inc(pool_acc, 1)
            gp.memset(ident[:, :], 0.0).then_inc(pool_set, 1)
            gp.wait_ge(pool_set, 1)
            gp.affine_select(out=ident[:, :], in_=ident[:, :], compare_op=ALU.not_equal, fill=1.0, base=0,
                             pattern=[[-1, 128]], channel_multiplier=1).then_inc(pool_set, 1)
            gp.memset(ones[:, :], 1.0).then_inc(pool_set, 1)
            gp.wait_ge(pool_set, 3)
            gp.iota(tok[:, 7:8].bitcast(I32), [[0, 1]], base=0, channel_multiplier=1).then_inc(pool_set, 1)

            def pair(n, last):
                pr = Pair(gp, n, start)
                for g in range(2):
                    for u in range(UNITS):
                        add_unit(gp, "pool", pr, g, u, last and g == 1)

            def big_layer(l):
                with gp.Fori(0, PAIRS - 1) as p:
                    pair(number(gp, l * PAIRS + p), False)
                pair(number(gp, l * PAIRS + PAIRS - 1), True)

            def group_divide(pr, h):
                g = h % GROUPS
                pr.wait(gdve_r, GROUPS, h + 1)
                if g == 0 and h > 0:
                    pr.wait(gpe_o, 8, 8 * (h // GROUPS))
                for j in range(JQ):
                    q = slice(j * QD, j * QD + QD)
                    gp.tensor_tensor(On[g * QD:g * QD + QD, j * 512:(j + 1) * 512], Oraw[q, h % 2, :], R[q, :],
                                     ALU.mult).then_inc(gpool_on, 1)

            big_layer(0)
            gp.wait_ge(dve_x, 8 * PAIRS + start["dve_x"])
            for k in KG:
                gp.memset(words(k[3 * QD:4 * QD, :]), 1.0).then_inc(pool_ones, 1)
            gp.wait_ge(pool_ones, GROUPS)
            gp.memset(V[:, :, :].rearrange("p t (g d) -> p (t g) d", g=GROUPS)[:, :, D1:QD], 1.0).then_inc(pool_ones, 1)
            group_divide(Pair(gp, 0, start), 0)
            with gp.Fori(0, ROUNDS - 1) as r:
                pr = Pair(gp, r, start)
                for h in range(1, 1 + GROUPS):
                    group_divide(pr, h)
            pr = Pair(gp, ROUNDS - 1, start)
            for h in range(1, GROUPS):
                group_divide(pr, h)
            gp.wait_ge(gdve_x, 8 * ROUNDS)
            for m, o in ((Q2[0], 64), (K2[0], 64), (K2[1], 0)):
                gp.memset(words(m[o:o + 64, :]), 0.0).then_inc(pool_clear, 1)
            with gp.Fori(0, BIG - 1) as l:
                big_layer(gp.snap(l + 1))

        @block.tensor
        def _(pe):
            for s in (pe_z, pe_pv, pe_o, pe_st):
                pe.sem_inc(s, 1)
            pe.wait_ge(pool_set, 3)
            pe.wait_ge(d_x, 32)
            for i in range(QT // 2):
                if i >= 4:
                    pe.wait_ge(act_set, i - 3)
                for k in range(4):
                    t, ct = 2 * i + k // 2, k % 2
                    last = pe.transpose(ST[i % 4][:, k * 128:(k + 1) * 128],
                                        x_land[t // XH][:, t % XH, ct * 128:(ct + 1) * 128], ident[:, :])
                last.then_inc(pe_set, 1)
            pe.wait_ge(d_in, 64)
            for t in range(KT):
                i = QT // 2 + t
                pe.wait_ge(act_set, i - 3)
                k = rows_of(t)
                for ct in range(CCT):
                    last = pe.transpose(ST[i % 4][:, ct * 128:ct * 128 + k],
                                        ctx_land[t][0:k, ct * 128:(ct + 1) * 128], ident[0:k, 0:k])
                last.then_inc(pe_set, 1)
            NSET = QT // 2 + KT + 1

            def project_kq(pr, n, first_waits):
                pr.wait(d_wkq, 32, 32 * (n + 1))
                for i in range(8):
                    if i < 4:
                        if i == 0:
                            first_waits()
                    else:
                        pr.wait(act_kq, 8, 8 * n + i - 3)
                    b = ST[i % 4]
                    if i < 4:
                        o, w = KCH[i]
                        for ct in range(CCT):
                            last = pe.matmul(b[:, 0:w], wk[:, ct, :], ctxT[:, ct, o:o + w],
                                             start=ct == 0, stop=ct == CCT - 1)
                    else:
                        j = i - 4
                        for ct in range(CT):
                            last = pe.matmul(b[:, :], wq[:, ct, :], xq[:, ct, j * 512:(j + 1) * 512],
                                             start=ct == 0, stop=ct == CT - 1)
                    last.then_inc(pe_kq, 1)
                    yield i

            def project_v(pr, n, first_waits):
                pr.wait(d_wv, 16, 16 * (n + 1))
                for i, (o, w) in enumerate(KCH):
                    first_waits(i)
                    w = min(w, NK - o)
                    for ct in range(CCT):
                        last = pe.matmul(ST[i][:, 0:w], wv[:, ct, :], ctxT[:, ct, o:o + w],
                                         start=ct == 0, stop=ct == CCT - 1)
                    last.then_inc(pe_v, 1)
                    yield i

            def transpose_v(pr, n):
                for i in range(4):
                    pr.wait(act_vraw, 4, 4 * n + min(i + 2, 4))
                    for t in range(4 * i, min(4 * i + 4, KT)):
                        k, c = rows_of(t), t - 4 * i
                        last = pe.transpose(ST[i][0:k, c * 128:(c + 1) * 128], rawV[:, t * 128:t * 128 + k], ident[:, :])
                    last.then_inc(pe_vt, 1)

            def s_tile(pr, g, i):
                b = g % 2
                if i == 0:
                    pr.wait(d_hi[b], 48, 48 * (g // 2 + 1))
                    pr.wait(dve_mrow, 2, g)
                    pr.wait(dve_s, 2 * SUNITS, g * SUNITS)
                if i >= 2:
                    pr.wait(dve_s, 2 * SUNITS, g * SUNITS + i - 1)
                qt, (o, w) = i // len(KCH), KCH[i % len(KCH)]
                pe.matmul(SS[i % 2][:, 0:w], Q2[b][:, qt * 128:(qt + 1) * 128], KS[b][:, o:o + w],
                          start=True, stop=True).then_inc(pe_s, 1)

            def transpose_max(pr, g):
                pr.wait(dve_m, 2, g + 1)
                pe.transpose(SS[0][0:QT, 0:128], negm[:, :], ident[:, :]).then_inc(pe_m, 1)

            def sums(pr, g, c2, alone=False):
                for jj in range(2):
                    wait_added(pr, g, (c2 + 1) * 2 * KT - 2 + jj, alone)
                pr.wait(dve_r, 4, 2 * g + c2)
                for jj in range(2):
                    last = pe.matmul(ZB[64 * jj:64 * jj + 64, :], ones[:, 0:64], acc[:, c2, jj, :],
                                     start=True, stop=True)
                last.then_inc(pe_z, 1)

            def attend(pr, g, bank_free, other):
                b = g % 2

                def scores(s, jj):
                    c2, t = s // KT, s % KT
                    k, u, j = rows_of(t), 2 * s + jj, 2 * c2 + jj
                    if u >= 4:
                        pr.wait(act_p, 2 * UNITS, g * UNITS + u - 3)
                    else:
                        bank_free(u)
                    bank = ST[u % 4][0:k, :]
                    pe.matmul(bank, K1[b][:, t * 128:t * 128 + k], Q1[b][:, j * 512:(j + 1) * 512],
                              start=True, stop=False)
                    pe.matmul(bank, K2[b][:, t * 128:t * 128 + k], Q2[b][:, j * 512:(j + 1) * 512],
                              start=False, stop=True).then_inc(pe_st, 1)

                def s_next(tiles, last=False):
                    for i in tiles if last else tiles[:1]:
                        s_tile(pr, other, i)
                    return tiles[1:]

                pr.wait(dve_lo, 16, 8 * (g + 1))
                pr.wait(d_m, 32, 16 * (g + 1))
                for jj in range(2):
                    scores(0, jj)
                if g == 1:
                    sums(pr, 0, 1)
                for s in range(STEPS):
                    c2, t = s // KT, s % KT
                    k = rows_of(t)
                    tiles = [] if other is None else list(s_units(s))
                    for jj in range(2):
                        if s + 1 < STEPS:
                            scores(s + 1, jj)
                        tiles = s_next(tiles)
                    pr.wait(act_p, 2 * UNITS, g * UNITS + 2 * s + 2)
                    if t == 0:
                        pr.wait(act_o, 4, 2 * g + c2)
                    for jj in range(2):
                        last = pe.matmul(OB[64 * jj:64 * jj + 64, :], V[0:k, t, 64 * b:64 * b + 64],
                                         P[0:k, (2 * s + jj) % NP, :], start=t == 0, stop=t == KT - 1)
                    last.then_inc(pe_pv, 1)
                    s_next(tiles, last=True)
                    if s == KT + 3:
                        sums(pr, g, 0, other is None)

            def output(pr, bank_free):
                pr.wait(d_wo, 16, 16)
                for i in range(CT * JQ):
                    ct, j = i % CT, i // CT
                    if i % CT == 0:
                        pr.wait(dve_on, 8, max(6, 5 + j))
                    if i >= 4:
                        pr.wait(dve_x, 8, i - 3)
                    else:
                        bank_free(i)
                    pe.matmul(ST[i % 4][:, :], wo[:, ct * 128:(ct + 1) * 128], On[:, j * 512:(j + 1) * 512],
                              start=True, stop=True).then_inc(pe_o, 1)

            def pair(l, p, last):
                pr = Pair(pe, number(pe, l * PAIRS + p), start)

                pr.wait(act_v, 4, 4)
                attend(pr, 0, lambda u: pr.wait(dve_x, 8, u - 3), 1)
                if last:
                    transpose_max(pr, 1)
                    attend(pr, 1, lambda u: None, None)
                    sums(pr, 1, 1, True)
                    output(pr, lambda i: pr.wait(act_p, 2 * UNITS, 2 * UNITS) if i == 0 else None)
                else:
                    for i in project_kq(pr, 1, lambda: pr.wait(act_p, 2 * UNITS, UNITS)):
                        if i == 0:
                            transpose_max(pr, 1)
                    attend(pr, 1, lambda u: pr.wait(act_kq, 8, 13 + u), 2)
                    for i in project_v(pr, 1, lambda i: pr.wait(act_p, 2 * UNITS, 2 * UNITS) if i == 0 else None):
                        if i == 0:
                            transpose_max(pr, 2)
                            sums(pr, 1, 1)
                    transpose_v(pr, 1)
                    output(pr, lambda i: pr.wait(act_v, 4, 5 + i))

            def big_layer(l):
                pe.wait_ge(act_set, NSET)
                pe.wait_ge(dve_x, number(pe, l * (8 * PAIRS) + start["dve_x"]))
                pr = Pair(pe, number(pe, l * PAIRS), start)
                for i in project_kq(pr, 0, lambda: None):
                    if i == 3:
                        pe.wait_ge(dve_xq, number(pe, l + 1))
                pe.wait_ge(d_ext, number(pe, l * 64 + 64))
                v = project_v(pr, 0, lambda i: pr.wait(act_kq, 8, 5 + i))
                for i in range(SUNITS):
                    s_tile(pr, 0, i)
                    if i % 8 == 7 and i < 40:
                        next(v, None)
                    if i == 47:
                        transpose_v(pr, 0)
                transpose_max(pr, 0)
                with pe.Fori(0, PAIRS - 1) as p:
                    pair(l, p, False)
                pair(l, PAIRS - 1, True)

            def group_project(pr, rnd):
                pr.wait(gd_wq, 16, 16 * (rnd + 1))
                for j in range(JQ):
                    for ct in range(CT):
                        last = pe.matmul(ST[j][:, :], gwq[:, ct, :], xq[:, ct, j * 512:(j + 1) * 512],
                                         start=ct == 0, stop=ct == CT - 1)
                    last.then_inc(gpe_q, 1)

            def group_s(pr, h, i):
                if i == 0:
                    pr.wait(gd_q, GROUPS * 64, 64 * (h + 1))
                    if h > 0:
                        pr.wait(gdve_mrow, GROUPS, h)
                if i >= len(GS):
                    pr.wait(gdve_s, GROUPS * SUNITS, h * SUNITS + i - len(GS) + 1)
                elif h > 0:
                    pr.wait(gdve_s, GROUPS * SUNITS, h * SUNITS)
                if i == 2 and h > 1:
                    pr.wait(gact_z, GROUPS, h - 1)
                qt, (o, w) = i // len(KCH), KCH[i % len(KCH)]
                pe.matmul(GS[i % len(GS)][:, 0:w], Q1[h % 2][0:MROW, qt * 128:(qt + 1) * 128], KG[h % GROUPS][0:MROW, o:o + w],
                          start=True, stop=True).then_inc(gpe_s, 1)

            def group_transpose_max(pr, h):
                pr.wait(gdve_m, GROUPS, h + 1)
                pe.transpose(SS[0][0:QT, 0:128], negm[:, :], ident[:, :]).then_inc(gpe_m, 1)

            def group_sums(pr, h):
                pr.wait(gact_o, GROUPS, h + 1)
                if h > 0:
                    pr.wait(gact_z, GROUPS, h)
                pe.matmul(ZB[:, :], sel[:, :], Oraw[:, h % 2, :], start=True, stop=True).then_inc(gpe_z, 1)

            def group_attend(pr, h, other, bank_free=lambda j: None):
                g = h % GROUPS

                def scores(t, j):
                    k = rows_of(t)
                    if t > 0:
                        pr.wait(gact_p, GROUPS * GUNITS, h * GUNITS + JQ * (t - 1) + j + 1)
                    pe.matmul(ST[j][0:k, :], KG[g][0:MROW + 1, t * 128:t * 128 + k],
                              Q1[h % 2][0:MROW + 1, j * 512:(j + 1) * 512], start=True, stop=True).then_inc(gpe_st, 1)

                pr.wait(gd_m, GROUPS * 16, 16 * (h + 1))
                for j in range(JQ):
                    bank_free(j)
                    scores(0, j)
                for t in range(KT):
                    k = rows_of(t)
                    tiles = g_s_units(t) if other else []
                    for j in range(JQ):
                        if t + 1 < KT:
                            scores(t + 1, j)
                        for i in tiles[:1]:
                            group_s(pr, h + 1, i)
                        tiles = tiles[1:]
                    for i in tiles[:1]:
                        group_s(pr, h + 1, i)
                    tiles = tiles[1:]
                    pr.wait(gact_p, GROUPS * GUNITS, h * GUNITS + JQ * (t + 1))
                    for j in range(JQ):
                        last = pe.matmul(OB[j * QD:j * QD + QD, :], V[0:k, t, g * QD:g * QD + QD],
                                         PG[(t * JQ + j) % len(PG)][0:k, :], start=t == 0, stop=t == KT - 1)
                    last.then_inc(gpe_pv, 1)
                    for i in tiles:
                        group_s(pr, h + 1, i)
                    if other and t == KT - 2:
                        group_transpose_max(pr, h + 1)
                group_sums(pr, h)

            def group_output(pr):
                pr.wait(gd_wo, 16, 16)
                pr.wait(gpool_on, 4 * GROUPS, 4 * GROUPS)
                for i in range(CT * JQ):
                    ct, j = i // JQ, i % JQ
                    if i >= 4:
                        pr.wait(gdve_x, 8, i - 3)
                    pe.matmul(ST[i % 4][:, :], gwo[:, ct * 128:(ct + 1) * 128], On[:, j * 512:(j + 1) * 512],
                              start=True, stop=True).then_inc(gpe_o, 1)
                pr.wait(gdve_x, 8, 8)

            def all_p(pr, h):
                pr.wait(gact_p, GROUPS * GUNITS, (h + 1) * GUNITS)

            def group_layer():
                pe.wait_ge(dve_x, 8 * PAIRS + start["dve_x"])
                for j in range(JQ):
                    pe.wait_ge(act_sq, j + 1)
                    for ct in range(CT):
                        last = pe.matmul(GB[j][:, :], ones[:, :], P[:, 2 * (j % 2) + ct, :],
                                         start=ct == 0, stop=ct == CT - 1)
                    last.then_inc(pe_sq, 1)
                pe.wait_ge(gd_load, 48)
                for banks, weights, done in ((ST, gwk, gpe_k), (GB, gwv, gpe_v)):
                    for i, (o, w) in enumerate(KCH):
                        if done is gpe_v:
                            pe.wait_ge(dve_var, i + 1)
                            w = min(w, NK - o)
                        for ct in range(CCT):
                            last = pe.matmul(banks[i][:, 0:w], weights[:, ct, :], ctxT[:, ct, o:o + w],
                                             start=ct == 0, stop=ct == CCT - 1)
                        last.then_inc(done, 1)
                pr = Pair(pe, 0, start)
                for i in range(4):
                    pe.wait_ge(gact_vraw, 4)
                    for t in range(4 * i, min(4 * i + 4, KT)):
                        k, c = rows_of(t), t - 4 * i
                        last = pe.transpose(GB[i][0:k, c * 128:(c + 1) * 128], rawV[:, t * 128:t * 128 + k], ident[:, :])
                    last.then_inc(gpe_vt, 1)
                pe.wait_ge(gdve_k, 4)
                pe.wait_ge(g_xq, 1)
                group_project(pr, 0)
                pe.wait_ge(gact_v, 4)
                pe.wait_ge(gd_k, 16 * 4 * GROUPS)
                pe.wait_ge(dve_sel, 4)
                for i in range(SUNITS):
                    group_s(pr, 0, i)
                group_transpose_max(pr, 0)
                group_attend(pr, 0, True)
                with pe.Fori(0, ROUNDS - 1) as r:
                    pr = Pair(pe, r, start)
                    group_attend(pr, 1, True)
                    group_attend(pr, 2, True)
                    all_p(pr, 2)
                    group_project(pr, 1)
                    group_attend(pr, 3, True, lambda j: pr.wait(gdve_q, 4, 5 + j))
                    group_attend(pr, 4, True)
                    all_p(pr, 4)
                    group_output(pr)
                pr = Pair(pe, ROUNDS - 1, start)
                group_attend(pr, 1, True)
                group_attend(pr, 2, True)
                group_attend(pr, 3, False)
                all_p(pr, 3)
                group_output(pr)
                pe.wait_ge(gd_bias, 16)

            big_layer(0)
            group_layer()
            with pe.Fori(0, BIG - 1) as l:
                big_layer(pe.snap(l + 1))

            pe.wait_ge(dve_x, BIG * PAIRS * 8 + start["dve_x"])
            for t in range(QT):
                if t >= 4:
                    pe.wait_ge(dve_out, t - 3)
                for ct in range(CT):
                    last = pe.transpose(ST[t % 4][:, ct * 128:(ct + 1) * 128], xacc[:, ct, t * 128:(t + 1) * 128],
                                        ident[:, :])
                last.then_inc(pe_out, 1)

        @block.scalar
        def _(act):
            act.sem_inc(act_o, 1)

            def copy(out, in_):
                return act.activation(out, in_, ACT.Copy)

            for i in range(QT // 2):
                act.wait_ge(pe_set, i + 1)
                copy(xacc[:, :, 2 * i * 128:(2 * i + 2) * 128].rearrange("p c (t q) -> p c t q", t=2),
                     ST[i % 4][:, :].rearrange("p (t c q) -> p c t q", t=2, c=2)).then_inc(act_set, 1)
            for t in range(KT):
                i = QT // 2 + t
                k = rows_of(t)
                act.wait_ge(pe_set, i + 1)
                copy(ctxT[:, :, t * 128:t * 128 + k],
                     ST[i % 4][:, :].rearrange("p (c k) -> p c k", c=CCT)[:, :, 0:k]).then_inc(act_set, 1)
            copy(ctxT[:, :, NK:KP], ST[(QT // 2 + KT - 1) % 4][:, :].rearrange("p (c k) -> p c k", c=CCT)
                 [:, :, KREST - 1:KREST]).then_inc(act_set, 1)

            def take_kq(pr, n, which):
                own = slice(0, 64)
                for i in which:
                    pr.wait(pe_kq, 8, 8 * n + i + 1)
                    raw, part, (o, w) = (rawK, K1[0], KCH[i]) if i < 4 else (rawQ, Q1[0], ((i - 4) * 512, 512))
                    ins = copy(part[own, o:o + w], ST[i % 4][own, 0:w])
                    if i % 4 == 3:
                        ins.then_inc(act_hi, 1)
                    copy(raw[:, o:o + w], ST[i % 4][:, 0:w]).then_inc(act_kq, 1)

            def odd_hi(dst, raw):
                copy(dst[1][64:128, :], raw[64:128, :]).then_inc(act_hi, 1)

            def raw_v(pr, n):
                for i, (o, w) in enumerate(KCH):
                    w = min(w, NK - o)
                    pr.wait(pe_v, 4, 4 * n + i + 1)
                    copy(rawV[:, o:o + w], ST[i][:, 0:w]).then_inc(act_vraw, 1)

            def tiles_v(pr, n):
                for i in range(4):
                    pr.wait(pe_vt, 4, 4 * n + i + 1)
                    c = min(4, KT - 4 * i)
                    k = rows_of(4 * i + c - 1)
                    copy(V[0:k, 4 * i:4 * i + c, :], ST[i][0:k, 0:c * 128].rearrange("k (t d) -> k t d", d=128))\
                        .then_inc(act_v, 1)

            def take_o(pr, g, c2):
                pr.wait(pe_pv, 2 * STEPS, g * STEPS + (c2 + 1) * KT)
                pr.wait(dve_on, 8, 4 * g)
                copy(Oraw[:, c2, :], OB[:, :]).then_inc(act_o, 1)

            def attend(pr, g, alone):
                for s in range(STEPS):
                    k = rows_of(s % KT)
                    for jj in range(2):
                        u = 2 * s + jj
                        pr.wait(pe_st, 2 * UNITS, g * UNITS + u + 1)
                        v = u - NP
                        if v >= 0:
                            pr.wait(pe_pv, 2 * STEPS, g * STEPS + v // 2 + 1)
                            wait_added(pr, g, v, alone)
                        elif u == 0:
                            pr.wait(pe_pv, 2 * STEPS, g * STEPS)
                            for done in (pool_acc, dve_acc):
                                pr.wait(done, 2 * UNITS, g * UNITS)
                        act.activation(P[0:k, u % NP, :], ST[u % 4][0:k, :], ACT.Exp, scale=SCALE).then_inc(act_p, 1)
                    if s == KT:
                        take_o(pr, g, 0)
                take_o(pr, g, 1)

            def pair(l, p, last):
                pr = Pair(act, number(act, l * PAIRS + p), start)
                attend(pr, 0, False)
                if not last:
                    pr.wait(dve_lo, 16, 16)
                    pr.wait(pe_st, 2 * UNITS, UNITS)
                    take_kq(pr, 1, range(0, 8))
                attend(pr, 1, last)
                if not last:
                    pr.wait(pe_st, 2 * UNITS, 2 * UNITS)
                    pr.wait(act_kq, 8, 16)
                    odd_hi(K1, rawK)
                    raw_v(pr, 1)
                    tiles_v(pr, 1)
                    odd_hi(Q1, rawQ)

            def big_layer(l):
                act.wait_ge(act_set, QT // 2 + KT + 1)
                act.wait_ge(dve_x, number(act, l * (8 * PAIRS) + start["dve_x"]))
                pr = Pair(act, number(act, l * PAIRS), start)
                act.wait_ge(dve_tok, number(act, l * TOK + TOK))
                take_kq(pr, 0, range(0, 4))
                act.wait_ge(d_ext, number(act, l * 64 + 64))
                take_kq(pr, 0, range(4, 8))
                raw_v(pr, 0)
                tiles_v(pr, 0)
                pr.wait(act_kq, 8, 8)
                odd_hi(K1, rawK)
                odd_hi(Q1, rawQ)
                with act.Fori(0, PAIRS - 1) as p:
                    pair(l, p, False)
                pair(l, PAIRS - 1, True)

            def group_hi(pr, rnd):
                for j in range(JQ):
                    pr.wait(gpe_q, 4, 4 * rnd + j + 1)
                    if rnd > 0 and j == 0:
                        pr.wait(gd_q, GROUPS * 64, GROUPS * 64)
                    copy(Q4hi[:, j * 512:(j + 1) * 512], ST[j][:, :]).then_inc(gact_q, 1)

            def group_take_z(pr, h):
                pr.wait(gpe_z, GROUPS, h + 1)
                if h > 0:
                    pr.wait(gdve_r, GROUPS, h)
                copy(Z, ZB[:, :]).then_inc(gact_z, 1)

            def group_attend(pr, h):
                for t in range(KT):
                    k = rows_of(t)
                    for j in range(JQ):
                        u = JQ * t + j
                        pr.wait(gpe_st, GROUPS * GUNITS, h * GUNITS + u + 1)
                        if u >= len(PG) or h > 0:
                            v = max(u - len(PG), -1) + 1
                            pr.wait(gpe_pv, GROUPS * KT, h * KT + -(-v // JQ))
                        act.activation(PG[u % len(PG)][0:k, :], ST[j][0:k, :], ACT.Exp, scale=SCALE1)\
                            .then_inc(gact_p, 1)
                pr.wait(gpe_pv, GROUPS * KT, (h + 1) * KT)
                if h > 1:
                    pr.wait(gpool_on, 4 * GROUPS, 4 * (h - 1))
                elif h == 1:
                    pr.wait(gpe_z, GROUPS, 1)
                copy(Oraw[:, h % 2, :], OB[:, :]).then_inc(gact_o, 1)
                group_take_z(pr, h)

            def group_layer():
                act.wait_ge(dve_x, 8 * PAIRS + start["dve_x"])
                for j in range(JQ):
                    if j >= 2:
                        act.wait_ge(pe_sq, j - 1)
                    for ct in range(CT):
                        last = act.activation(P[:, 2 * (j % 2) + ct, :], xacc[:, ct, j * 512:(j + 1) * 512], ACT.Square)
                    last.then_inc(act_sq, 1)
                act.wait_ge(pe_sq, JQ)
                for i, (o, w) in enumerate(KCH):
                    act.wait_ge(gpe_k, i + 1)
                    copy(K4hi[:, o:o + w], ST[i][:, 0:w]).then_inc(gact_k, 1)
                for i, (o, w) in enumerate(KCH):
                    w = min(w, NK - o)
                    act.wait_ge(gpe_v, i + 1)
                    copy(rawV[:, o:o + w], GB[i][:, 0:w]).then_inc(gact_vraw, 1)
                for i in range(4):
                    act.wait_ge(gpe_vt, i + 1)
                    c = min(4, KT - 4 * i)
                    k = rows_of(4 * i + c - 1)
                    copy(V[0:k, 4 * i:4 * i + c, :].rearrange("k t (g d) -> k t g d", g=GROUPS)[:, :, :, 0:D1],
                         GB[i][0:k, 0:c * 128].rearrange("k (t g d) -> k t g d", t=c, g=GROUPS)[:, :, :, 0:D1])\
                        .then_inc(gact_v, 1)
                act.wait_ge(dve_inv, JQ)
                act.activation(On[:, :], On[:, :], ACT.Sqrt).then_inc(act_rms, 1)
                pr = Pair(act, 0, start)
                group_hi(pr, 0)
                act.wait_ge(gd_k, 16 * 4 * GROUPS)
                group_attend(pr, 0)
                with act.Fori(0, ROUNDS - 1) as r:
                    pr = Pair(act, r, start)
                    group_attend(pr, 1)
                    group_attend(pr, 2)
                    group_hi(pr, 1)
                    group_attend(pr, 3)
                    group_attend(pr, 4)
                pr = Pair(act, ROUNDS - 1, start)
                for h in range(1, GROUPS):
                    group_attend(pr, h)
                act.wait_ge(gdve_x, 8 * ROUNDS)

            big_layer(0)
            group_layer()
            with act.Fori(0, BIG - 1) as l:
                big_layer(act.snap(l + 1))

        @block.vector
        def _(dve):
            for s in (dve_s, dve_mrow, dve_r, dve_x, dve_on, dve_m, dve_acc):
                dve.sem_inc(s, start[s.name])
            for b in range(2):
                o = 64 * (1 - b)
                for m in (Q2[b], K2[b], KS[b]):
                    dve.memset(words(m[o:o + 64, :]), 0.0).then_inc(dve_zero, 1)
            dve.wait_ge(d_m, 16)
            m = xq[0:2, 0, :]
            dve.tensor_scalar(m, m, -1.0, 1.0, ALU.mult, ALU.add).then_inc(dve_set, 1)
            dve.wait_ge(dve_set, 1)
            dve.tensor_scalar(m, m, -SUPPRESS / SCALE, None, ALU.mult).then_inc(dve_bias, 1)
            dve.wait_ge(dve_bias, 1)
            dve.tensor_copy(Q1[0][0:2, :], m).then_inc(dve_bias, 1)
            dve.wait_ge(dve_bias, 2)
            dve.tensor_tensor(Q1[1][0:2, :], m, Q1[0][0:2, :], ALU.subtract).then_inc(dve_bias, 1)
            dve.wait_ge(pool_set, 4)
            dve.tensor_scalar(first_row[:, :], tok[:, 7:8].bitcast(I32), 0.0, None, ALU.is_equal).then_inc(dve_set, 1)
            dve.wait_ge(d_biasrow, 128)

            def lo_part(pr, g, i):
                b = g % 2
                own, other = slice(64 * b, 64 * b + 64), slice(64 * (1 - b), 64 * (1 - b) + 64)
                pr.wait(act_hi, 4, 2 * g + 1 + i // 4)
                pr.wait(act_kq, 8, 8 * (g // 2) + 4 * (i // 4 + 1))
                if i < 4:
                    c = slice(KCH[i][0], sum(KCH[i]))
                    ins = dve.tensor_tensor(K2[b][own, c], rawK[own, c], K1[b][own, c], ALU.subtract)
                else:
                    c = slice((i - 4) * 512, (i - 3) * 512)
                    ins = dve.tensor_tensor(Q1[b][other, c], rawQ[own, c], Q1[b][own, c], ALU.subtract)
                ins.then_inc(dve_lo, 1)

            def s_max(pr, g, i):
                w = KCH[i % len(KCH)][1]
                if i == 0:
                    pr.wait(dve_m, 2, g)
                pr.wait(pe_s, 2 * SUNITS, g * SUNITS + i + 1)
                dve.tensor_reduce(mpart[:, i // len(KCH), i % len(KCH):i % len(KCH) + 1], SS[i % 2][:, 0:w],
                                  AX.X, ALU.max).then_inc(dve_s, 1)

            def head_max(pr, g):
                pr.wait(dve_s, 2 * SUNITS, (g + 1) * SUNITS)
                dve.tensor_reduce(negm[:, :], mpart[:, :, :], AX.X, ALU.max, negate=True).then_inc(dve_m, 1)

            def max_row(pr, g):
                pr.wait(pe_m, 2, g + 1)
                pr.wait(d_m, 32, 16 * g)
                dve.tensor_copy(mrow[:, :], SS[0][0:QT, 0:128]).then_inc(dve_mrow, 1)

            def reciprocals(pr, g, c2, piece, pieces=8):
                w = 512 // pieces
                q = slice(piece * w, piece * w + w)
                if piece == 0:
                    pr.wait(dve_on, 8, 4 * g + 2 * c2)
                    pr.wait(pe_z, 4, 2 * g + c2 + 1)
                ins = dve.reciprocal(R[:, q], ZB[:, q])
                if piece == pieces - 1:
                    ins.then_inc(dve_r, 1)

            def divide(pr, g, c2, chunks=(0, 1)):
                b = g % 2
                pr.wait(dve_r, 4, 2 * g + c2 + 1)
                pr.wait(act_o, 4, 2 * g + c2 + 1)
                if g == 0 and c2 == 0:
                    pr.wait(pe_o, 8, 0)
                for jj in chunks:
                    j, r = 2 * c2 + jj, slice(64 * jj, 64 * jj + 64)
                    dve.tensor_tensor(On[64 * b:64 * b + 64, j * 512:(j + 1) * 512], Oraw[r, c2, :], R[r, :],
                                      ALU.mult).then_inc(dve_on, 1)

            def normalise(pr, g, c2):
                reciprocals(pr, g, c2, 0, 1)
                divide(pr, g, c2)

            def attend(pr, g, other):
                for s in range(STEPS):
                    if other is not None and 4 <= s < 12:
                        lo_part(pr, other, s - 4)
                    if other is not None:
                        for i in s_units(s):
                            s_max(pr, other, i)
                    for u in (2 * s, 2 * s + 1):
                        add_unit(dve, "dve", pr, g, u, other is None)
                    if KT + 3 <= s < KT + 11:
                        reciprocals(pr, g, 0, s - KT - 3)
                    elif s >= KT + 11:
                        divide(pr, g, 0, (s - KT - 11,))

            def add_output(pr):
                for i in range(CT * JQ):
                    ct, j = i % CT, i // CT
                    pr.wait(pe_o, 8, i + 1)
                    x = xacc[:, ct, j * 512:(j + 1) * 512]
                    dve.tensor_tensor(x, ST[i % 4][:, :], x, ALU.add).then_inc(dve_x, 1)

            def pair(l, p, last):
                pr = Pair(dve, number(dve, l * PAIRS + p), start)
                attend(pr, 0, 1)
                head_max(pr, 1)
                max_row(pr, 1)
                normalise(pr, 0, 1)
                attend(pr, 1, None if last else 2)
                if not last:
                    head_max(pr, 2)
                    max_row(pr, 2)
                normalise(pr, 1, 1)
                add_output(pr)

            dve.wait_ge(act_set, QT // 2 + KT + 1)
            def big_layer(l):
                dve.wait_ge(d_layer, number(dve, l * 48 + 48))
                steps = number(dve, l * TOK)

                def link(ins, k):
                    ins.then_inc(dve_tok, 1)
                    dve.wait_ge(dve_tok, steps + k)
                key, hit, hit2 = rawK[0:NROWS, :], rawQ[0:NROWS, 0:KP], On[0:NROWS, 0:KP]
                link(dve.tensor_copy(tok[:, 0:4], tok_i[:, :]), 1)
                link(dve.tensor_scalar(R[0:NROWS, 0:4], tok[:, 0:4], 0.0, float(NK), ALU.is_lt, ALU.mult), 2)
                link(dve.tensor_tensor(tok[:, 0:4], tok[:, 0:4], R[0:NROWS, 0:4], ALU.add), 3)
                link(dve.tensor_scalar(hit, key, tok[:, 2:3], None, ALU.is_equal), 4)
                link(dve.scalar_tensor_tensor(hit, key, tok[:, 3:4], hit, ALU.is_equal, ALU.max), 5)
                link(dve.tensor_scalar(hit, hit, -1.0, 1.0, ALU.mult, ALU.add), 6)
                link(dve.tensor_scalar(hit2, key, tok[:, 0:1], None, ALU.is_equal), 7)
                link(dve.scalar_tensor_tensor(hit2, key, tok[:, 1:2], hit2, ALU.is_equal, ALU.max), 8)
                link(dve.tensor_tensor(hit2, hit2, hit, ALU.mult), 9)
                link(dve.tensor_scalar(K1[1][0:NROWS, :], hit2, first_row[:, 0:1], None, ALU.add), TOK)
                dve.tensor_copy(xq[:, :, :], xacc[:, :, :]).then_inc(dve_xq, 1)
                dve.wait_ge(dve_xq, number(dve, l + 1))
                for ct in range(CT):
                    last = dve.tensor_scalar(xacc[:, ct, :], xacc[:, ct, :], bo[:, ct:ct + 1], None, ALU.add)
                last.then_inc(dve_bo, 1)
                dve.wait_ge(dve_bo, number(dve, l + 1))
                pr = Pair(dve, number(dve, l * PAIRS), start)
                for i in range(8):
                    lo_part(pr, 0, i)
                for i in range(SUNITS):
                    s_max(pr, 0, i)
                head_max(pr, 0)
                max_row(pr, 0)
                with dve.Fori(0, PAIRS - 1) as p:
                    pair(l, p, False)
                pair(l, PAIRS - 1, True)

            def group_lo(pr, rnd):
                for j in range(JQ):
                    q = slice(j * 512, (j + 1) * 512)
                    pr.wait(gact_q, 4, 4 * rnd + j + 1)
                    dve.tensor_tensor(Q4lo[:, q], ST[j][:, :], Q4hi[:, q], ALU.subtract).then_inc(gdve_q, 1)

            def group_s_max(pr, h, i):
                w = KCH[i % len(KCH)][1]
                if i == 0 and h > 0:
                    pr.wait(gdve_m, GROUPS, h)
                pr.wait(gpe_s, GROUPS * SUNITS, h * SUNITS + i + 1)
                dve.tensor_reduce(mpart[:, i // len(KCH), i % len(KCH):i % len(KCH) + 1], GS[i % len(GS)][:, 0:w],
                                  AX.X, ALU.max).then_inc(gdve_s, 1)

            def group_max(pr, h):
                pr.wait(gdve_s, GROUPS * SUNITS, (h + 1) * SUNITS)
                dve.tensor_reduce(negm[:, :], mpart[:, :, :], AX.X, ALU.max, negate=True).then_inc(gdve_m, 1)
                pr.wait(gpe_m, GROUPS, h + 1)
                if h > 0:
                    pr.wait(gd_m, 16 * GROUPS, 16 * h)
                dve.tensor_copy(mrow[:, :], SS[0][0:QT, 0:128]).then_inc(gdve_mrow, 1)

            def group_reciprocals(pr, h):
                pr.wait(gact_z, GROUPS, h + 1)
                if h > 0:
                    pr.wait(gpool_on, 4 * GROUPS, 4 * h)
                dve.reciprocal(R[:, :], Z[:, :]).then_inc(gdve_r, 1)

            def group_attend(pr, h, other):
                for t in range(KT):
                    for i in g_s_units(t) if other else []:
                        group_s_max(pr, h + 1, i)
                if other:
                    group_max(pr, h + 1)
                group_reciprocals(pr, h)

            def group_add(pr):
                for i in range(CT * JQ):
                    ct, j = i // JQ, i % JQ
                    pr.wait(gpe_o, 8, i + 1)
                    x = xacc[:, ct, j * 512:(j + 1) * 512]
                    dve.tensor_tensor(x, ST[i % 4][:, :], x, ALU.add).then_inc(gdve_x, 1)

            def group_layer():
                for j in range(GROUPS):
                    dve.tensor_scalar(sel[:, j * QD:(j + 1) * QD], ones[:, 0:QD], ident[:, j * QD + D1:j * QD + D1 + 1],
                                      None, ALU.mult).then_inc(dve_sel, 1)
                for j in range(JQ):
                    dve.wait_ge(pe_sq, j + 1)
                    dve.tensor_scalar(rawQ[:, j * 512:(j + 1) * 512], GB[j][:, :], 1.0 / C, EPS, ALU.mult, ALU.add)\
                        .then_inc(dve_var, 1)
                for j in range(JQ):
                    q = slice(j * 512, (j + 1) * 512)
                    dve.wait_ge(dve_var, j + 1)
                    dve.reciprocal(On[:, q], rawQ[:, q]).then_inc(dve_inv, 1)
                    o, w = KCH[j]
                    dve.wait_ge(gact_k, j + 1)
                    dve.tensor_tensor(K4lo[:, o:o + w], ST[j][:, 0:w], K4hi[:, o:o + w], ALU.subtract).then_inc(gdve_k, 1)
                dve.wait_ge(act_rms, 1)
                dve.wait_ge(gd_load, 48)
                for ct in range(CT):
                    last = dve.scalar_tensor_tensor(xq[:, ct, :], xacc[:, ct, :], nw[:, ct:ct + 1], On[:, :],
                                                    ALU.mult, ALU.mult)
                last.then_inc(g_xq, 1)
                pr = Pair(dve, 0, start)
                group_lo(pr, 0)
                for i in range(SUNITS):
                    group_s_max(pr, 0, i)
                group_max(pr, 0)
                group_attend(pr, 0, True)
                with dve.Fori(0, ROUNDS - 1) as r:
                    pr = Pair(dve, r, start)
                    group_attend(pr, 1, True)
                    group_attend(pr, 2, True)
                    group_lo(pr, 1)
                    group_attend(pr, 3, True)
                    group_attend(pr, 4, True)
                    group_add(pr)
                pr = Pair(dve, ROUNDS - 1, start)
                for h in range(1, GROUPS):
                    group_attend(pr, h, h < GROUPS - 1)
                group_add(pr)
                dve.wait_ge(gdve_x, 8 * ROUNDS)

            big_layer(0)
            group_layer()
            with dve.Fori(0, BIG - 1) as l:
                big_layer(dve.snap(l + 1))

            for t in range(QT):
                dve.wait_ge(pe_out, t + 1)
                dve.tensor_copy(x_out[:, t, :], ST[t % 4][:, 0:C]).then_inc(dve_out, 1)


def kernel(**inp):
    import concourse.bacc as bacc
    from concourse.bass_utils import run_bass_kernel_spmd as run

    big = ["L0_xattn_", "L2_xattn_", "L3_xattn_"]
    f = np.float32
    wq = np.zeros((BIG, C, HEADS, D), f)
    wk = np.zeros((BIG, CC, HEADS, D), f)
    wv = np.zeros((BIG, CC, HEADS, D), f)
    wo = np.zeros((BIG, HEADS, D, C), f)
    bo = np.zeros((BIG, C), f)
    tok = np.full((BIG, NROWS, 4), NONE, np.int32)
    for l, k in enumerate(big):
        wq[l] = np.asarray(inp[k + "Wq"]).reshape(C, HEADS, D)
        wk[l] = np.asarray(inp[k + "Wk"]).reshape(CC, HEADS, D)
        wv[l] = np.asarray(inp[k + "Wv"]).reshape(CC, HEADS, D)
        wo[l] = np.asarray(inp[k + "Wo"]).reshape(HEADS, D, C)
        bo[l] = np.asarray(inp[k + "bo"])
        A, B = np.asarray(inp[k + "token_indices_A"]), np.asarray(inp[k + "token_indices_B"])
        tok[l, 1:3, 0:2] = A
        tok[l, 1:3, 2:4] = B
        tok[l, 3:5, 0:2] = B

    def quadrants(w):
        out = np.zeros((w.shape[0], GROUPS, QD), f)
        out[:, :, :D1] = w
        return np.ascontiguousarray(out.reshape(-1, P128, GROUPS * QD).transpose(1, 0, 2))

    gq = np.asarray(inp["L1_xattn_wq"]).reshape(C, GROUPS, ROUNDS, D1)
    gwq = np.stack([quadrants(gq[:, :, r]) for r in range(ROUNDS)] + [quadrants(gq[:, :, 0])])
    gwo = np.zeros((ROUNDS, GROUPS, QD, C), f)
    gwo[:, :, :D1] = np.asarray(inp["L1_xattn_wo"]).reshape(GROUPS, ROUNDS, D1, C).transpose(1, 0, 2, 3)

    def columns(w, n):
        w = w.reshape(BIG, n, P128, PAIRS, 2 * D).transpose(0, 3, 2, 1, 4).reshape(BIG * PAIRS, P128, n, 2 * D)
        return np.ascontiguousarray(np.concatenate([w, w[:1]]))

    def vectors(v):
        return np.ascontiguousarray(v.reshape(BIG, CT, P128).transpose(0, 2, 1))

    wo = wo.reshape(BIG * PAIRS, 2 * D, C)
    arrays = {
        "x": np.ascontiguousarray(np.asarray(inp["x"])[0]),
        "ctx": np.ascontiguousarray(np.asarray(inp["ctx_2048"])[0]),
        "mask": np.stack([np.asarray(inp["mask_S_fk1"]), np.asarray(inp["mask_S_fk0"])]),
        "wq": columns(wq, CT), "wk": columns(wk, CCT), "wv": columns(wv, CCT),
        "wo": np.ascontiguousarray(np.concatenate([wo, wo[:1]])),
        "bo": vectors(bo), "tok": tok,
        "gwk": quadrants(np.asarray(inp["L1_xattn_wk"]).reshape(CC, GROUPS, D1)),
        "gwv": quadrants(np.asarray(inp["L1_xattn_wv"]).reshape(CC, GROUPS, D1)),
        "gwq": gwq, "gwo": gwo.reshape(ROUNDS, P128, C),
        "nw": np.ascontiguousarray(np.asarray(inp["L1_xattn_norm_w"]).reshape(CT, P128).T),
        "key": np.tile(np.minimum(np.arange(KP), NK - 1).astype(f), (NROWS, 1)),
    }
    nc = bacc.Bacc("TRN2", target_bir_lowering=False, num_devices=1)
    aps = {k: nc.dram_tensor(f"in_{k}", v.shape, mybir.dt.from_np(v.dtype), kind="ExternalInput").ap()
           for k, v in arrays.items()}
    aps["out"] = nc.dram_tensor("out", (NQ, C), F32, kind="ExternalOutput").ap()
    attention_layers(nc, aps)
    r = run(nc, [{f"in_{k}": v for k, v in arrays.items()}], core_ids=[0])
    return r.results[0]["out"].reshape(1, NQ, C)
```
